# Optimizing a Trainium2 kernel written in Bass

```python
import numpy as np
import jax
import jax.numpy as jnp

def _softmax(x, axis=-1):
    return jax.nn.softmax(x, axis=axis)

def _gelu(x):
    return jax.nn.gelu(x, approximate=True)

def _silu(x):
    return jax.nn.silu(x)

def _sigmoid(x):
    return jax.nn.sigmoid(x)

def _layernorm(x, axis=-1, eps=1e-05):
    m = jnp.mean(x, axis=axis, keepdims=True)
    v = jnp.var(x, axis=axis, keepdims=True)
    return (x - m) / jnp.sqrt(v + eps)

def _scatter_add(tgt, idx, src, axis=0):
    return tgt.at[idx].add(src)

def _segment_sum(src, seg, n):
    return jax.ops.segment_sum(src, seg, n)
kernel_name = 'mk_conv_seq_d2_conv_nchw192_r2_a1e8ef'

def setup_inputs(seed: int=0):
    np.random.seed(seed)
    _w = jnp.asarray

    def _rec_inputs():
        import jax
        import jax.numpy as jnp
        _gk = jax.random.key(seed)
        x = -4.65e-05 + 0.9999 * jax.random.normal(jax.random.fold_in(_gk, 1), (4, 96, 128, 128), jnp.float32)
        return x
    x = _rec_inputs()

    def _L0_conv_setup():
        import jax, jax.numpy as jnp
        import numpy as np
        DIM = 96
        HEADS = 6
        WS = 8
        SS = 4
        EPS = 1e-05

        def _build_mask(H, W, ws, ss):
            img = np.zeros((H, W), np.float32)
            cnt = 0
            for h in (slice(0, -ws), slice(-ws, -ss), slice(-ss, None)):
                for w in (slice(0, -ws), slice(-ws, -ss), slice(-ss, None)):
                    img[h, w] = cnt
                    cnt += 1
            mw = img.reshape(H // ws, ws, W // ws, ws).transpose(0, 2, 1, 3).reshape(-1, ws * ws)
            diff = mw[:, None, :] - mw[:, :, None]
            return jnp.asarray(np.where(diff != 0, -100.0, 0.0).astype(np.float32))

        def _ln(x, w, b):
            m = x.mean(-1, keepdims=True)
            v = ((x - m) ** 2).mean(-1, keepdims=True)
            return (x - m) / jnp.sqrt(v + EPS) * w + b
        key = jax.random.key(seed)
        ks = jax.random.split(key, 8)
        C, HID = (DIM, 4 * DIM)
        s = 0.05
        return {'x': jax.random.normal(ks[0], (4, C, 128, 128), jnp.float32), 'norm1_w': jnp.ones((C,), jnp.float32), 'norm1_b': jnp.zeros((C,), jnp.float32), 'qkv_w': jax.random.normal(ks[1], (3 * C, C), jnp.float32) * s, 'qkv_b': jax.random.normal(ks[2], (3 * C,), jnp.float32) * s, 'proj_w': jax.random.normal(ks[3], (C, C), jnp.float32) * s, 'proj_b': jax.random.normal(ks[4], (C,), jnp.float32) * s, 'norm2_w': jnp.ones((C,), jnp.float32), 'norm2_b': jnp.zeros((C,), jnp.float32), 'mlp_w1': jax.random.normal(ks[5], (HID, C), jnp.float32) * s, 'mlp_b1': jax.random.normal(ks[6], (HID,), jnp.float32) * s, 'mlp_w2': jax.random.normal(ks[7], (C, HID), jnp.float32) * s, 'mlp_b2': jnp.zeros((C,), jnp.float32)}
    _L0_conv_all = _L0_conv_setup()
    _L0_conv_in = {k: v for k, v in _L0_conv_all.items() if k in ('norm1_w', 'norm1_b', 'qkv_w', 'qkv_b', 'proj_w', 'proj_b', 'norm2_w', 'norm2_b', 'mlp_w1', 'mlp_b1', 'mlp_w2', 'mlp_b2')}
    del _L0_conv_all

    def _L1_conv_setup():
        import jax, jax.numpy as jnp
        import numpy as np
        REPARAM_OFFSET = 2.0 ** (-18)
        PEDESTAL = REPARAM_OFFSET ** 2
        BETA_MIN = 1e-06
        BOUND_BETA = (BETA_MIN + PEDESTAL) ** 0.5
        BOUND_GAMMA = PEDESTAL ** 0.5
        INVERSE = False

        def _nn_init(v):
            return jnp.sqrt(jnp.maximum(v + PEDESTAL, PEDESTAL))

        def _nn_reparam(v, bound):
            return jnp.square(jnp.maximum(v, bound)) - PEDESTAL
        key = jax.random.key(seed)
        N, C, H, W = (4, 96, 128, 128)
        x = jax.random.normal(key, (N, C, H, W), dtype=jnp.float32)
        beta = _nn_init(jnp.ones((C,), dtype=jnp.float32))
        gamma = _nn_init(0.1 * jnp.eye(C, dtype=jnp.float32))
        return {'x': x, 'beta': beta, 'gamma': gamma}
    _L1_conv_all = _L1_conv_setup()
    _L1_conv_in = {k: v for k, v in _L1_conv_all.items() if k in ('beta', 'gamma')}
    del _L1_conv_all
    return {'x': x, 'L0_conv_norm1_w': _L0_conv_in['norm1_w'], 'L0_conv_norm1_b': _L0_conv_in['norm1_b'], 'L0_conv_qkv_w': _L0_conv_in['qkv_w'], 'L0_conv_qkv_b': _L0_conv_in['qkv_b'], 'L0_conv_proj_w': _L0_conv_in['proj_w'], 'L0_conv_proj_b': _L0_conv_in['proj_b'], 'L0_conv_norm2_w': _L0_conv_in['norm2_w'], 'L0_conv_norm2_b': _L0_conv_in['norm2_b'], 'L0_conv_mlp_w1': _L0_conv_in['mlp_w1'], 'L0_conv_mlp_b1': _L0_conv_in['mlp_b1'], 'L0_conv_mlp_w2': _L0_conv_in['mlp_w2'], 'L0_conv_mlp_b2': _L0_conv_in['mlp_b2'], 'L1_conv_beta': _L1_conv_in['beta'], 'L1_conv_gamma': _L1_conv_in['gamma']}

def reference(x, L0_conv_norm1_w, L0_conv_norm1_b, L0_conv_qkv_w, L0_conv_qkv_b, L0_conv_proj_w, L0_conv_proj_b, L0_conv_norm2_w, L0_conv_norm2_b, L0_conv_mlp_w1, L0_conv_mlp_b1, L0_conv_mlp_w2, L0_conv_mlp_b2, L1_conv_beta, L1_conv_gamma):
    import jax
    import jax.numpy as jnp

    def _L0_conv_ref(x, norm1_w, norm1_b, qkv_w, qkv_b, proj_w, proj_b, norm2_w, norm2_b, mlp_w1, mlp_b1, mlp_w2, mlp_b2):
        import jax, jax.numpy as jnp
        import numpy as np
        DIM = 96
        HEADS = 6
        WS = 8
        SS = 4
        EPS = 1e-05

        def _build_mask(H, W, ws, ss):
            img = np.zeros((H, W), np.float32)
            cnt = 0
            for h in (slice(0, -ws), slice(-ws, -ss), slice(-ss, None)):
                for w in (slice(0, -ws), slice(-ws, -ss), slice(-ss, None)):
                    img[h, w] = cnt
                    cnt += 1
            mw = img.reshape(H // ws, ws, W // ws, ws).transpose(0, 2, 1, 3).reshape(-1, ws * ws)
            diff = mw[:, None, :] - mw[:, :, None]
            return jnp.asarray(np.where(diff != 0, -100.0, 0.0).astype(np.float32))

        def _ln(x, w, b):
            m = x.mean(-1, keepdims=True)
            v = ((x - m) ** 2).mean(-1, keepdims=True)
            return (x - m) / jnp.sqrt(v + EPS) * w + b
        B, C, H, W = x.shape
        ws, ss = (WS, SS)
        heads = HEADS
        hd = C // heads
        N = ws * ws
        x = jnp.transpose(x, (0, 2, 3, 1))
        shortcut = x
        y = _ln(x, norm1_w, norm1_b)
        y = jnp.roll(y, (-ss, -ss), axis=(1, 2))
        y = y.reshape(B, H // ws, ws, W // ws, ws, C).transpose(0, 1, 3, 2, 4, 5).reshape(-1, N, C)
        qkv = y @ qkv_w.T + qkv_b
        qkv = qkv.reshape(-1, N, 3, heads, hd).transpose(2, 0, 3, 1, 4)
        q = qkv[0] * hd ** (-0.5)
        k = qkv[1]
        v = qkv[2]
        attn = jnp.einsum('bhnd,bhmd->bhnm', q, k)
        mask = _build_mask(H, W, ws, ss)
        nW = mask.shape[0]
        attn = attn.reshape(B, nW, heads, N, N) + mask[None, :, None]
        attn = jax.nn.softmax(attn, axis=-1).reshape(-1, heads, N, N)
        out = jnp.einsum('bhnm,bhmd->bnhd', attn, v).reshape(-1, N, C)
        out = out @ proj_w.T + proj_b
        out = out.reshape(B, H // ws, W // ws, ws, ws, C).transpose(0, 1, 3, 2, 4, 5).reshape(B, H, W, C)
        out = jnp.roll(out, (ss, ss), axis=(1, 2))
        x = shortcut + out
        h1 = jax.nn.gelu(_ln(x, norm2_w, norm2_b) @ mlp_w1.T + mlp_b1, approximate=False)
        x = x + (h1 @ mlp_w2.T + mlp_b2)
        return jnp.transpose(x, (0, 3, 1, 2))

    def _L1_conv_ref(x, beta, gamma):
        import jax, jax.numpy as jnp
        import numpy as np
        REPARAM_OFFSET = 2.0 ** (-18)
        PEDESTAL = REPARAM_OFFSET ** 2
        BETA_MIN = 1e-06
        BOUND_BETA = (BETA_MIN + PEDESTAL) ** 0.5
        BOUND_GAMMA = PEDESTAL ** 0.5
        INVERSE = False

        def _nn_init(v):
            return jnp.sqrt(jnp.maximum(v + PEDESTAL, PEDESTAL))

        def _nn_reparam(v, bound):
            return jnp.square(jnp.maximum(v, bound)) - PEDESTAL
        beta_eff = _nn_reparam(beta, BOUND_BETA)
        gamma_eff = _nn_reparam(gamma, BOUND_GAMMA)
        x2 = x * x
        denom_sq = jnp.einsum('nchw,ic->nihw', x2, gamma_eff)
        denom_sq = denom_sq + beta_eff[None, :, None, None]
        norm = jnp.sqrt(denom_sq) if INVERSE else jax.lax.rsqrt(denom_sq)
        return x * norm

    def _gn(v, G=32, eps=1e-05):
        B_, C_, H_, W_ = v.shape
        g = v.reshape(B_, G, C_ // G, H_, W_)
        m = jnp.mean(g, axis=(2, 3, 4), keepdims=True)
        s = jnp.var(g, axis=(2, 3, 4), keepdims=True)
        return ((g - m) / jnp.sqrt(s + eps)).reshape(v.shape)

    def _ln_c(v, eps=1e-06):
        m = jnp.mean(v, axis=1, keepdims=True)
        s = jnp.var(v, axis=1, keepdims=True)
        return (v - m) / jnp.sqrt(s + eps)

    def _ln_t(v, eps=1e-05):
        m = jnp.mean(v, axis=-1, keepdims=True)
        s = jnp.var(v, axis=-1, keepdims=True)
        return (v - m) / jnp.sqrt(s + eps)

    def _to_tokens(v):
        B_, C_, H_, W_ = v.shape
        return v.reshape(B_, C_, H_ * W_).transpose(0, 2, 1)

    def _from_tokens(t, like):
        B_, C_, H_, W_ = like.shape
        return t.transpose(0, 2, 1).reshape(B_, C_, H_, W_)
    x = _L0_conv_ref(x, L0_conv_norm1_w, L0_conv_norm1_b, L0_conv_qkv_w, L0_conv_qkv_b, L0_conv_proj_w, L0_conv_proj_b, L0_conv_norm2_w, L0_conv_norm2_b, L0_conv_mlp_w1, L0_conv_mlp_b1, L0_conv_mlp_w2, L0_conv_mlp_b2)
    x = _L1_conv_ref(x, L1_conv_beta, L1_conv_gamma)
    return x

_drawn_inputs = setup_inputs


def setup_inputs(seed=0):
    import zlib

    import numpy as np

    out = dict(_drawn_inputs(seed))
    spreads = {'L0_conv_norm1_w': (1.0, 0.6),
     'L0_conv_norm1_b': (0.0, 0.383),
     'L0_conv_norm2_w': (1.0, 0.2),
     'L0_conv_norm2_b': (0.0, 0.267),
     'L0_conv_mlp_b2': (0.0, 0.1),
     'L1_conv_beta': (1.0, 0.2)}
    factors = {}
    for name, (base, spread) in spreads.items():
        noise = np.random.default_rng([zlib.crc32(name.encode()), seed]).standard_normal(out[name].shape)
        drawn = base * np.exp(spread * noise) if base else spread * noise
        out[name] = jnp.asarray(drawn.astype(out[name].dtype))
    for name, factor in factors.items():
        out[name] = (out[name] * factor).astype(out[name].dtype)
    return out
```

```python
import concourse.bass as bass
from concourse import mybir
from contextlib import ExitStack

N_IMAGES, DIM, HEIGHT, WIDTH = 4, 96, 128, 128
HEADS, WIN, SHIFT = 6, 8, 4
HEAD_DIM = DIM // HEADS
HIDDEN = 4 * DIM
HID_CHUNKS = HIDDEN // 128
ROWS = HEIGHT // WIN
WINDOWS = WIDTH // WIN
TOKENS = WIN * WIN
UNIT = WINDOWS * TOKENS
UNITS = N_IMAGES * ROWS
HALF = UNIT // 2
PAIRS = WINDOWS // 2
HALF_PAIRS = PAIRS // 2
HEAD_PAIRS = HEADS // 2
CHUNKS = HALF // 128
MASK_ROWS = 8
LN_EPS = 1e-5
PEDESTAL = 2.0 ** -36
BOUND_BETA = (1e-6 + PEDESTAL) ** 0.5
BOUND_GAMMA = PEDESTAL ** 0.5
MASKED = -100.0
LAG = 2


def window_block(nc, x, qmask, kmask, ident, head_mask, ones_pair, norm1_w, norm1_b, qkv_t, qkv_b,
                 proj_t, proj_b, norm2_w, norm2_b, w1_t, b1, w2_t, b2, beta, gamma_t, out):
    f32 = mybir.dt.float32
    ALU = mybir.AluOpType
    ACT = mybir.ActivationFunctionType
    AX = mybir.AxisListType

    ctx = ExitStack()
    with ctx:
        def sb(name, shape, dt=f32):
            return ctx.enter_context(nc.sbuf_tensor(name, shape, dt))

        def bank(name):
            return ctx.enter_context(nc.psum_tensor(name, [128, 512], f32))

        def sem(name):
            return ctx.enter_context(nc.semaphore(name))

        ident_sb = sb("ident_sb", [128, 128])
        head_mask_sb = sb("head_mask_sb", [DIM, HEADS])
        ones_pair_sb = sb("ones_pair_sb", [128, 32])
        qkv_raw = sb("qkv_raw", [DIM, 3 * DIM])
        w1_raw = sb("w1_raw", [DIM, HIDDEN])
        norm_cols = sb("norm_cols", [DIM, 4])
        b2_col = sb("b2_col", [DIM, 1])
        wq = sb("wq", [DIM + 1, DIM])
        wk = sb("wk", [DIM + 1, DIM])
        wv = sb("wv", [128, 2, HEAD_PAIRS, HEAD_DIM])
        wproj = sb("wproj", [DIM + 1, DIM])
        w1 = sb("w1", [DIM + 1, HIDDEN])
        w2 = sb("w2", [128, HID_CHUNKS, DIM])
        wgdn = sb("wgdn", [DIM + 1, DIM])
        gdn_raw = sb("gdn_raw", [DIM + 1, DIM])
        qkv_bias = sb("qkv_bias", [DIM + 1, 3 * DIM])
        b1_row = sb("b1_row", [DIM + 1, HIDDEN])
        eps_col = sb("eps_col", [128, 1])

        x_ext = sb("x_ext", [DIM, 2, WIN, WIDTH + SHIFT])
        o_ext = sb("o_ext", [DIM, 2, WIN, WIDTH + SHIFT])
        stats = [sb(f"stats{n}", [128, 2 * CHUNKS, 6]) for n in (1, 2)]
        moments = [sb(f"moments{n}", [128, 2 * CHUNKS, 2]) for n in (1, 2)]
        log_var = [sb(f"log_var{n}", [128, 2 * CHUNKS]) for n in (1, 2)]
        rstd = [sb(f"rstd{n}", [128, 2 * CHUNKS]) for n in (1, 2)]
        y_tok = [sb(f"y_tok{n}", [128, 2 * CHUNKS, DIM]) for n in (1, 2)]
        y1 = sb("y1", [128, UNIT])
        y2 = sb("y2", [DIM + 1, UNIT])
        q = sb("q", [128, 2, UNIT])
        k = sb("k", [DIM, UNIT])
        k_block = sb("k_block", [128, 2, WINDOWS, HEADS, TOKENS])
        v_block = sb("v_block", [128, 2, WINDOWS, HEAD_PAIRS, 32])
        row_max = sb("row_max", [128, 2, HEADS])
        shifted = sb("shifted", [128, 2, HEADS, TOKENS])
        probs = sb("probs", [128, 4, HEADS, TOKENS])
        probs_t = sb("probs_t", [128, 2, HEAD_PAIRS, HALF_PAIRS, 128])
        log_sum = sb("log_sum", [DIM, HALF])
        inv_sum = sb("inv_sum", [DIM, HALF])
        attended = sb("attended", [DIM + 1, UNIT])
        x2 = sb("x2", [DIM, 2, UNIT])
        hidden = sb("hidden", [128, HID_CHUNKS, UNIT])
        x3 = sb("x3", [DIM, UNIT])
        x3_sq = sb("x3_sq", [DIM + 1, UNIT])
        log_den = sb("log_den", [DIM, UNIT])
        inv_den = sb("inv_den", [DIM, UNIT])

        score_bank = bank("score_bank")
        probs_t_bank = bank("probs_t_bank")
        pv_bank = bank("pv_bank")
        sum_bank = bank("sum_bank")
        turn_banks = [bank("turn_bank0"), bank("turn_bank1")]
        mm_banks = [bank("mm_bank0"), bank("mm_bank1")]

        waits_passed = sem("waits_passed")
        consts_loaded = sem("consts_loaded")
        key_mask_loaded = sem("key_mask_loaded")
        cleared = sem("cleared")
        pads_cleared = sem("pads_cleared")
        weights_folded = sem("weights_folded")
        bias_products = sem("bias_products")
        x_loaded = [sem("x_loaded0"), sem("x_loaded1")]
        out_stored = [sem("out_stored0"), sem("out_stored1")]
        x_wrapped = sem("x_wrapped")
        out_wrapped = sem("out_wrapped")
        x_turned = [sem("x_turned1"), sem("x_turned2")]
        stats_made = [sem("stats_made1"), sem("stats_made2")]
        moments_ready = [sem("moments_ready1"), sem("moments_ready2")]
        log_var_made = [sem("log_var_made1"), sem("log_var_made2")]
        rstd_ready = [sem("rstd_ready1"), sem("rstd_ready2")]
        normed = [sem("normed1"), sem("normed2")]
        y_turned = [sem("y_turned1"), sem("y_turned2")]
        y_ready = [sem("y_ready1"), sem("y_ready2")]
        qk_made = sem("qk_made")
        qk_ready = sem("qk_ready")
        key_block_v = sem("key_block_v")
        key_block_p = sem("key_block_p")
        v_made = sem("v_made")
        v_ready = sem("v_ready")
        scores_made = sem("scores_made")
        max_ready = sem("max_ready")
        scores_shifted = sem("scores_shifted")
        probs_ready = sem("probs_ready")
        probs_turned = sem("probs_turned")
        probs_t_ready = sem("probs_t_ready")
        pv_made = sem("pv_made")
        sums_made = sem("sums_made")
        log_sum_made = sem("log_sum_made")
        inv_sum_ready = sem("inv_sum_ready")
        attended_ready = sem("attended_ready")
        proj_made = sem("proj_made")
        x2_ready = sem("x2_ready")
        mlp1_made = sem("mlp1_made")
        gelu_ready = sem("gelu_ready")
        mlp2_made = sem("mlp2_made")
        x3_ready = sem("x3_ready")
        sq_ready = sem("sq_ready")
        den_made = sem("den_made")
        log_den_made = sem("log_den_made")
        inv_den_ready = sem("inv_den_ready")
        out_ready = sem("out_ready")

        UNIT_OF = {"load": 1, "attend": 0, "finish": -1, "settle": -2}

        def stages_of(i):
            return [stage for stage, ahead in UNIT_OF.items() if 0 <= i + ahead < UNITS]

        def iterations(engine, body):
            first, last = 2, UNITS - 2
            trips = (last - first) // 2
            for i in range(-1, first):
                body(i, i % 2, stages_of(i))
            with engine.Fori(0, trips) as trip:
                for n in range(2):
                    body(2 * trip + (first + n), n, list(UNIT_OF))
            for i in range(first + 2 * trips, UNITS + 2):
                body(i, i % 2, stages_of(i))

        def wait(engine, semaphore, count):
            if not isinstance(count, int) or count > 0:
                engine.wait_ge(semaphore, count)

        def wait_alone(engine, semaphore, count):
            engine.wait_ge(semaphore, count)
            engine.sem_inc(waits_passed, 1)

        MM_ITEMS = [
            ("proj0", "finish", x2_ready, 2, 1), ("v0", "attend", v_ready, 2, 1),
            ("mlp2_0", "settle", x3_ready, 2, 1), ("v1", "attend", v_ready, 2, 2),
            ("mlp2_1", "settle", x3_ready, 2, 2), ("proj1", "finish", x2_ready, 2, 2),
            ("den0", "settle", log_den_made, 2, 1), ("den1", "settle", log_den_made, 2, 2),
            *((f"mlp1_{n}", "finish", gelu_ready, 2 * HID_CHUNKS, n + 1) for n in range(2 * HID_CHUNKS)),
            ("q0", "load", qk_ready, 4, 1), ("k0", "load", qk_ready, 4, 2),
            ("q1", "load", qk_ready, 4, 3), ("k1", "load", qk_ready, 4, 4),
        ]
        MM_AT = {item[0]: at for at, item in enumerate(MM_ITEMS)}
        def mm_bank(name):
            return mm_banks[MM_AT[name] % 2]

        def mm_bank_emptied(name, i, stages):
            def among(items, i, stages):
                for at, (other, stage, semaphore, per_unit, own) in reversed(items):
                    if at % 2 == MM_AT[name] % 2 and stage in stages:
                        return semaphore, per_unit * (i + UNIT_OF[stage]) + own
                return None
            found = among(list(enumerate(MM_ITEMS))[:MM_AT[name]], i, stages)
            if found is None:
                before = stages_of(i - 1) if isinstance(i, int) else list(UNIT_OF)
                found = among(list(enumerate(MM_ITEMS)), i - 1, before)
            return found

        def windows_of(tile, half):
            first = SHIFT + half * (WIDTH // 2)
            return tile[:, :, first:first + WIDTH // 2].rearrange("c r (n w) -> c n r w", w=WIN)

        def in_windows(flat):
            return flat.rearrange("c (n r w) -> c n r w", r=WIN, w=WIN)

        def half_of(tile, half):
            return tile[:, half * HALF:(half + 1) * HALF]

        block = ctx.enter_context(nc.Block())

        @block.sync
        def _(sp):
            for dst, src in ((ident_sb[:, :], ident), (head_mask_sb[:, :], head_mask),
                             (ones_pair_sb[:, :], ones_pair), (qkv_raw[:, :], qkv_t),
                             (w1_raw[:, :], w1_t), (norm_cols[:, 0:1], norm1_w),
                             (norm_cols[:, 1:2], norm1_b), (norm_cols[:, 2:3], norm2_w),
                             (norm_cols[:, 3:4], norm2_b), (b2_col[:, :], b2),
                             (wproj[0:DIM, :], proj_t), (wproj[DIM:DIM + 1, :], proj_b),
                             (w2[:, :, :], w2_t.rearrange("(c p) n -> p c n", p=128)),
                             (gdn_raw[0:DIM, :], gamma_t), (gdn_raw[DIM:DIM + 1, :], beta),
                             (qkv_bias[DIM:DIM + 1, :], qkv_b), (b1_row[DIM:DIM + 1, :], b1)):
                sp.dma_start(dst, src).then_inc(consts_loaded, 16)

            def load_x(unit, slot):
                image, row = unit // ROWS, unit % ROWS
                for n, first in enumerate((row * WIN + SHIFT, ((row + 1) % ROWS) * WIN)):
                    sp.dma_start(x_ext[:, slot, n * SHIFT:(n + 1) * SHIFT, 0:WIDTH],
                                 x[bass.ds(image, 1), :, bass.ds(first, SHIFT), :]
                                 .rearrange("n c h w -> (n c) h w")).then_inc(x_loaded[slot], 16)
                sp.dma_start(q[DIM:DIM + MASK_ROWS, slot, :],
                             qmask[bass.ds(row, 1), :, :].rearrange("n m t -> (n m) t"))\
                    .then_inc(x_loaded[slot], 16)

            def store_out(unit, slot):
                image, row = unit // ROWS, unit % ROWS
                for n, first in enumerate((row * WIN + SHIFT, ((row + 1) % ROWS) * WIN)):
                    sp.dma_start(out[bass.ds(image, 1), :, bass.ds(first, SHIFT), :]
                                 .rearrange("n c h w -> (n c) h w"),
                                 o_ext[:, slot, n * SHIFT:(n + 1) * SHIFT, 0:WIDTH])\
                        .then_inc(out_stored[slot], 16)

            def body(i, parity, stages):
                load, attend, finish, settle = (stage in stages for stage in UNIT_OF)
                if load:
                    if isinstance(i, int) and i < 1:
                        if i == -1:
                            sp.wait_ge(pads_cleared, 1)
                    else:
                        wait_alone(sp, x2_ready, 2 * i)
                        wait_alone(sp, scores_made, PAIRS * i)
                    load_x(i + 1, 1 - parity)
                if settle:
                    wait_alone(sp, out_wrapped, i - 1)
                    store_out(i - 2, parity)

            iterations(sp, body)
            for slot in range(2):
                sp.wait_ge(out_stored[slot], 32 * (UNITS // 2))

        @block.gpsimd
        def _(pool):
            nc.gpsimd.memset(q[DIM:128, :, :], 0.0).then_inc(pads_cleared, 1)
            nc.gpsimd.memset(k_block[DIM:128, :, :, :, :], 0.0).then_inc(pads_cleared, 1)
            pool.wait_ge(pads_cleared, 2)
            for slot in range(2):
                pool.dma_start(k_block[DIM:DIM + MASK_ROWS, slot, :, :, :]
                               .rearrange("m n h t -> m (n h t)"), kmask).then_inc(key_mask_loaded, 16)

            def body(i, parity, stages):
                load, attend, finish, settle = (stage in stages for stage in UNIT_OF)
                slot = 1 - parity
                if load:
                    unit = i + 1
                    wait_alone(pool, x_loaded[slot], 48 * (unit // 2 + 1))
                    nc.gpsimd.tensor_copy(x_ext[:, slot, :, WIDTH:WIDTH + SHIFT],
                                          x_ext[:, slot, :, 0:SHIFT]).then_inc(x_wrapped, 1)
                    if isinstance(i, int) and i == -1:
                        pool.wait_ge(consts_loaded, 16 * 17)
                if load:
                    for half in range(2):
                        wait_alone(pool, qk_ready, 4 * (i + 1) + 2 * half + 2)
                        for h in range(HEADS // 2):
                            made = nc.gpsimd.tensor_scalar(
                                k_block[0:DIM, slot, half * PAIRS:(half + 1) * PAIRS, h, :],
                                half_of(k, half).rearrange("c (n t) -> c n t", t=TOKENS),
                                head_mask_sb[:, h:h + 1], 1.0, ALU.mult, ALU.mult)
                        made.then_inc(key_block_p, 1)
                if settle:
                    wait_alone(pool, out_ready, 2 * (i - 1))
                    nc.gpsimd.tensor_copy(o_ext[:, parity, :, 0:SHIFT],
                                          o_ext[:, parity, :, WIDTH:WIDTH + SHIFT])\
                        .then_inc(out_wrapped, 1)

            iterations(pool, body)

        @block.scalar
        def _(act):
            def rstd_of(ln, unit, half):
                act.wait_ge(moments_ready[ln], 2 * unit + half + 1)
                cols = slice(half * CHUNKS, (half + 1) * CHUNKS)
                nc.scalar.activation(log_var[ln][:, cols], moments[ln][:, cols, 1], ACT.Ln,
                                     bias=eps_col[:, :]).then_inc(log_var_made[ln], 1)
                act.wait_ge(log_var_made[ln], 2 * unit + half + 1)
                nc.scalar.activation(rstd[ln][:, cols], log_var[ln][:, cols], ACT.Exp, scale=-0.5)\
                    .then_inc(rstd_ready[ln], 1)

            def y_copy(ln, unit, half):
                act.wait_ge(y_turned[ln], 2 * unit + half + 1)
                if ln == 0:
                    rows = slice(half * CHUNKS, (half + 1) * CHUNKS)
                    dst = in_windows(y1[0:DIM, :])[:, :, rows, :]
                    src = turn_banks[half][0:DIM, :].rearrange("c (r n w) -> c n r w", r=CHUNKS, w=WIN)
                else:
                    dst, src = half_of(y2[0:DIM, :], half), turn_banks[half][0:DIM, :]
                nc.scalar.activation(dst, src, ACT.Copy).then_inc(y_ready[ln], 1)

            def qk_copy(unit, slot, half):
                for n, dst in enumerate((q[0:DIM, slot, :], k[:, :])):
                    act.wait_ge(qk_made, 4 * unit + 2 * half + n + 1)
                    if n == 1:
                        wait(act, key_block_v, 2 * unit + half - 1)
                        wait(act, key_block_p, 2 * unit + half - 1)
                    nc.scalar.activation(half_of(dst, half), mm_bank(f"{'qk'[n]}{half}")[0:DIM, :],
                                         ACT.Copy).then_inc(qk_ready, 1)

            def softmax_exp(unit, j):
                pair = PAIRS * unit + j
                act.wait_ge(scores_shifted, pair + 1)
                wait(act, probs_turned, pair - 3)
                nc.scalar.activation(probs[:, j % 4, :, :], shifted[:, j % 2, :, :], ACT.Exp)\
                    .then_inc(probs_ready, 1)

            def probs_t_copy(unit, j):
                act.wait_ge(probs_turned, PAIRS * unit + j + 1)
                nc.scalar.activation(probs_t[:, j // HALF_PAIRS, :, j % HALF_PAIRS, :],
                                     probs_t_bank[:, 0:HEAD_PAIRS * 128]
                                     .rearrange("k (p t) -> k p t", p=HEAD_PAIRS), ACT.Copy)\
                    .then_inc(probs_t_ready, 1)

            def inverse_sums(unit, half):
                at = 2 * unit + half
                act.wait_ge(sums_made, at + 1)
                nc.scalar.activation(log_sum[:, :], sum_bank[0:DIM, :], ACT.Ln).then_inc(log_sum_made, 1)
                act.wait_ge(log_sum_made, at + 1)
                wait(act, attended_ready, at)
                nc.scalar.activation(inv_sum[:, :], log_sum[:, :], ACT.Exp, scale=-1.0)\
                    .then_inc(inv_sum_ready, 1)

            def gelus(unit, half):
                for chunk in range(HID_CHUNKS):
                    n = half * HID_CHUNKS + chunk
                    act.wait_ge(mlp1_made, 2 * HID_CHUNKS * unit + n + 1)
                    nc.scalar.activation(half_of(hidden[:, chunk, :], half), mm_bank(f"mlp1_{n}")[:, :],
                                         ACT.Gelu).then_inc(gelu_ready, 1)

            def squares(unit, half):
                act.wait_ge(x3_ready, 2 * unit + half + 1)
                nc.scalar.activation(half_of(x3_sq[0:DIM, :], half), half_of(x3, half), ACT.Square)\
                    .then_inc(sq_ready, 1)

            def inverse_denominators(unit, half):
                act.wait_ge(den_made, 2 * unit + half + 1)
                nc.scalar.activation(half_of(log_den, half), mm_bank(f"den{half}")[0:DIM, :], ACT.Ln)\
                    .then_inc(log_den_made, 1)
                act.wait_ge(log_den_made, 2 * unit + half + 1)
                nc.scalar.activation(half_of(inv_den, half), half_of(log_den, half), ACT.Exp, scale=-0.5)\
                    .then_inc(inv_den_ready, 1)

            def use_ln_and_exp():
                nc.scalar.preload_act_table_set("natural_log_exp_and_others")

            use_ln_and_exp()

            def body(i, parity, stages):
                load, attend, finish, settle = (stage in stages for stage in UNIT_OF)
                for j in range(PAIRS):
                    if j < LAG:
                        if finish:
                            probs_t_copy(i - 1, PAIRS - LAG + j)
                    elif attend:
                        probs_t_copy(i, j - LAG)
                    if finish and j == 2:
                        y_copy(1, i - 1, 0)
                    if finish and j == 5:
                        gelus(i - 1, 1)
                        use_ln_and_exp()
                    if attend:
                        softmax_exp(i, j)
                    if j == 1:
                        if settle:
                            squares(i - 2, 0)
                        if finish:
                            rstd_of(1, i - 1, 0)
                            inverse_sums(i - 1, 1)
                    if settle and j == 2:
                        squares(i - 2, 1)
                    if j == 3:
                        if settle:
                            inverse_denominators(i - 2, 0)
                        if finish:
                            rstd_of(1, i - 1, 1)
                        if settle:
                            inverse_denominators(i - 2, 1)
                    if j == 4:
                        if load:
                            rstd_of(0, i + 1, 0)
                        if finish:
                            gelus(i - 1, 0)
                            y_copy(1, i - 1, 1)
                    if j == 5:
                        if load:
                            rstd_of(0, i + 1, 1)
                        if attend:
                            inverse_sums(i, 0)
                        if load:
                            y_copy(0, i + 1, 0)
                    if load and j == 6:
                        y_copy(0, i + 1, 1)
                        qk_copy(i + 1, 1 - parity, 0)
                    if load and j == 7:
                        qk_copy(i + 1, 1 - parity, 1)

            iterations(act, body)

        @block.vector
        def _(dve):
            nc.vector.memset(y1[DIM:128, :], 0.0).then_inc(cleared, 1)
            nc.vector.memset(wv[DIM:128, :, :, :], 0.0).then_inc(cleared, 1)
            nc.vector.memset(v_block[:, :, :, :, :], 0.0).then_inc(cleared, 1)
            nc.vector.memset(y2[DIM:DIM + 1, :], 1.0).then_inc(cleared, 1)
            nc.vector.memset(attended[DIM:DIM + 1, :], 1.0).then_inc(cleared, 1)
            nc.vector.memset(x3_sq[DIM:DIM + 1, :], 1.0).then_inc(cleared, 1)
            nc.vector.memset(eps_col[:, :], LN_EPS).then_inc(cleared, 1)
            dve.wait_ge(cleared, 7)
            nc.vector.memset(y1[DIM:DIM + 1, :], 1.0).then_inc(cleared, 1)
            dve.wait_ge(consts_loaded, 16 * 17)
            head_scale = HEAD_DIM ** -0.5
            nc.vector.tensor_scalar(wq[0:DIM, :], qkv_raw[:, 0:DIM], norm_cols[:, 0:1], head_scale,
                                    ALU.mult, ALU.mult)
            nc.vector.tensor_scalar(wk[0:DIM, :], qkv_raw[:, DIM:2 * DIM], norm_cols[:, 0:1], None,
                                    ALU.mult)
            def even_odd(row):
                return row.rearrange("c (p e d) -> c e p d", e=2, d=HEAD_DIM)
            nc.vector.tensor_scalar(wv[0:DIM, :, :, :], even_odd(qkv_raw[:, 2 * DIM:3 * DIM]),
                                    norm_cols[:, 0:1], None, ALU.mult)
            nc.vector.tensor_scalar(w1[0:DIM, :], w1_raw[:, :], norm_cols[:, 2:3], None, ALU.mult)
            nc.vector.tensor_scalar(gdn_raw[0:DIM, :], gdn_raw[0:DIM, :], BOUND_GAMMA, None, ALU.max)\
                .then_inc(weights_folded, 1)
            nc.vector.tensor_scalar(gdn_raw[DIM:DIM + 1, :], gdn_raw[DIM:DIM + 1, :], BOUND_BETA, None,
                                    ALU.max).then_inc(weights_folded, 1)
            dve.wait_ge(weights_folded, 2)
            nc.vector.tensor_tensor(wgdn[:, :], gdn_raw[:, :], gdn_raw[:, :], ALU.mult)\
                .then_inc(weights_folded, 1)
            dve.wait_ge(weights_folded, 3)
            nc.vector.tensor_scalar(wgdn[:, :], wgdn[:, :], -PEDESTAL, None, ALU.add)
            dve.wait_ge(bias_products, 1)
            row = slice(DIM, DIM + 1)
            qkv_shift = score_bank[row, 0:3 * DIM]
            nc.vector.tensor_tensor(qkv_bias[row, :], qkv_shift, qkv_bias[row, :], ALU.add)\
                .then_inc(weights_folded, 1)
            nc.vector.tensor_tensor(w1[row, :], pv_bank[row, 0:HIDDEN], b1_row[row, :], ALU.add)
            dve.wait_ge(weights_folded, 4)
            nc.vector.tensor_scalar(wq[row, :], qkv_bias[row, 0:DIM], head_scale, None, ALU.mult)
            nc.vector.tensor_copy(wk[row, :], qkv_bias[row, DIM:2 * DIM])
            nc.vector.tensor_copy(wv[row, :, :, :], even_odd(qkv_bias[row, 2 * DIM:3 * DIM]))\
                .then_inc(weights_folded, 1)

            def statistics(ln, unit, half):
                at = 2 * unit + half
                dve.wait_ge(x_turned[ln], at + 1)
                for c in range(CHUNKS):
                    made = nc.vector.bn_stats(stats[ln][:, half * CHUNKS + c, :],
                                              turn_banks[half][:, c * DIM:(c + 1) * DIM])
                made.then_inc(stats_made[ln], 1)
                wait_alone(dve, stats_made[ln], at + 1)
                for c in range(CHUNKS):
                    made = nc.vector.bn_aggr(moments[ln][:, half * CHUNKS + c, :],
                                             stats[ln][:, half * CHUNKS + c, :])
                made.then_inc(moments_ready[ln], 1)

            def normalise(ln, unit, half):
                dve.wait_ge(rstd_ready[ln], 2 * unit + half + 1)
                for c in range(CHUNKS):
                    at = half * CHUNKS + c
                    made = nc.vector.tensor_scalar(y_tok[ln][:, at, :],
                                                   turn_banks[half][:, c * DIM:(c + 1) * DIM],
                                                   moments[ln][:, at, 0:1], rstd[ln][:, at:at + 1],
                                                   ALU.subtract, ALU.mult)
                made.then_inc(normed[ln], 1)

            def key_blocks(unit, slot, half):
                dve.wait_ge(qk_ready, 4 * unit + 2 * half + 2)
                for h in range(HEADS // 2, HEADS):
                    made = nc.vector.tensor_scalar(
                        k_block[0:DIM, slot, half * PAIRS:(half + 1) * PAIRS, h, :],
                        half_of(k, half).rearrange("c (n t) -> c n t", t=TOKENS),
                        head_mask_sb[:, h:h + 1], None, ALU.mult)
                made.then_inc(key_block_v, 1)

            def v_blocks(unit, slot, half):
                dve.wait_ge(v_made, 2 * unit + half + 1)
                for e in range(2):
                    rows = slice(64 * e, 64 * e + 64)
                    made = nc.vector.tensor_copy(
                        v_block[rows, slot, half * PAIRS:(half + 1) * PAIRS, :,
                                HEAD_DIM * e:HEAD_DIM * (e + 1)],
                        mm_bank(f"v{half}")[rows, 0:PAIRS * HEAD_PAIRS * HEAD_DIM]
                        .rearrange("k (n p d) -> k n p d", n=PAIRS, p=HEAD_PAIRS))
                made.then_inc(v_ready, 1)

            def shift_scores(unit, j):
                pair = PAIRS * unit + j
                dve.wait_ge(scores_made, pair + 1)
                scores = score_bank[:, 0:HEADS * TOKENS].rearrange("t (h k) -> t h k", h=HEADS)
                nc.vector.tensor_reduce(row_max[:, j % 2, :], scores, op=ALU.max, axis=AX.X)\
                    .then_inc(max_ready, 1)
                dve.wait_ge(max_ready, pair + 1)
                wait(dve, probs_ready, pair - 1)
                nc.vector.tensor_tensor(shifted[:, j % 2, :, :], scores,
                                        row_max[:, j % 2, :].unsqueeze(2)
                                        .broadcast_to([128, HEADS, TOKENS]), ALU.subtract)\
                    .then_inc(scores_shifted, 1)

            def divide(unit, half):
                dve.wait_ge(inv_sum_ready, 2 * unit + half + 1)
                dve.wait_ge(pv_made, PAIRS * unit + HALF_PAIRS * (half + 1))
                nc.vector.tensor_tensor(half_of(attended[0:DIM, :], half), pv_bank[0:DIM, :],
                                        inv_sum[:, :], ALU.mult).then_inc(attended_ready, 1)

            def first_residual(unit, slot, half):
                dve.wait_ge(proj_made, 2 * unit + half + 1)
                nc.vector.tensor_tensor(in_windows(half_of(x2[:, slot, :], half)),
                                        in_windows(mm_bank(f"proj{half}")[0:DIM, :]),
                                        windows_of(x_ext[:, slot, :, :], half), ALU.add)\
                    .then_inc(x2_ready, 1)

            def second_residual(unit, slot, half):
                dve.wait_ge(mlp2_made, 2 * unit + half + 1)
                nc.vector.scalar_tensor_tensor(half_of(x3, half), mm_bank(f"mlp2_{half}")[0:DIM, :],
                                               b2_col[:, :], half_of(x2[:, slot, :], half), ALU.add, ALU.add)\
                    .then_inc(x3_ready, 1)

            def outputs(unit, slot, half):
                dve.wait_ge(inv_den_ready, 2 * unit + half + 1)
                wait(dve, out_stored[slot], 32 * (unit // 2))
                nc.vector.tensor_tensor(windows_of(o_ext[:, slot, :, :], half),
                                        in_windows(half_of(x3, half)), in_windows(half_of(inv_den, half)),
                                        ALU.mult).then_inc(out_ready, 1)

            def body(i, parity, stages):
                load, attend, finish, settle = (stage in stages for stage in UNIT_OF)
                other = 1 - parity
                for j in range(PAIRS):
                    if attend:
                        shift_scores(i, j)
                    if j == 0:
                        if finish:
                            first_residual(i - 1, other, 0)
                        if attend:
                            v_blocks(i, parity, 0)
                    if j == 1:
                        if settle:
                            second_residual(i - 2, parity, 0)
                        if finish:
                            statistics(1, i - 1, 0)
                        if attend:
                            v_blocks(i, parity, 1)
                        if finish:
                            normalise(1, i - 1, 0)
                    if j == 2:
                        if finish:
                            divide(i - 1, 1)
                        if settle:
                            second_residual(i - 2, parity, 1)
                        if finish:
                            first_residual(i - 1, other, 1)
                    if j == 3:
                        if finish:
                            statistics(1, i - 1, 1)
                        if settle:
                            outputs(i - 2, parity, 0)
                        if load:
                            statistics(0, i + 1, 0)
                    if j == 4:
                        if finish:
                            normalise(1, i - 1, 1)
                        if load:
                            normalise(0, i + 1, 0)
                        if settle:
                            outputs(i - 2, parity, 1)
                        if load:
                            statistics(0, i + 1, 1)
                    if load and j == 5:
                        normalise(0, i + 1, 1)
                    if j == 6:
                        if attend:
                            divide(i, 0)
                        if load:
                            key_blocks(i + 1, other, 0)
                    if load and j == 7:
                        key_blocks(i + 1, other, 1)

            iterations(dve, body)

        @block.tensor
        def _(pe):
            pe.wait_ge(consts_loaded, 16 * 17)
            row = slice(DIM, DIM + 1)
            nc.tensor.matmul(score_bank[row, 0:3 * DIM], norm_cols[:, 1:2], qkv_raw[:, :],
                             start=True, stop=True)
            nc.tensor.matmul(pv_bank[row, 0:HIDDEN], norm_cols[:, 3:4], w1_raw[:, :],
                             start=True, stop=True).then_inc(bias_products, 1)
            pe.wait_ge(weights_folded, 5)
            pe.wait_ge(cleared, 8)
            pe.wait_ge(pads_cleared, 2)
            pe.wait_ge(key_mask_loaded, 32)

            def mm_wait(name, i, stages):
                found = mm_bank_emptied(name, i, stages)
                if found is not None:
                    wait(pe, *found)

            def turn_in(ln, unit, slot, half, bank_emptied):
                if ln == 0:
                    pe.wait_ge(x_wrapped, unit + 1)
                else:
                    pe.wait_ge(x2_ready, 2 * unit + half + 1)
                if bank_emptied is not None:
                    wait(pe, *bank_emptied)
                for c in range(CHUNKS):
                    if ln == 0:
                        chunk = x_ext[:, slot, half * CHUNKS + c, SHIFT:SHIFT + WIDTH]
                    else:
                        chunk = half_of(x2[:, slot, :], half)[:, c * 128:(c + 1) * 128]
                    made = nc.tensor.transpose(turn_banks[half][:, c * DIM:(c + 1) * DIM], chunk,
                                               ident_sb[0:DIM, 0:DIM])
                made.then_inc(x_turned[ln], 1)

            def turn_out(ln, unit, half):
                pe.wait_ge(normed[ln], 2 * unit + half + 1)
                for c in range(CHUNKS):
                    made = nc.tensor.transpose(turn_banks[half][0:DIM, c * 128:(c + 1) * 128],
                                               y_tok[ln][:, half * CHUNKS + c, :], ident_sb[:, :])
                made.then_inc(y_turned[ln], 1)

            def project_qk(name, w, unit, half, i, stages):
                pe.wait_ge(y_ready[0], 2 * unit + 2)
                mm_wait(name, i, stages)
                nc.tensor.matmul(mm_bank(name)[0:DIM, :], w[:, :], half_of(y1[0:DIM + 1, :], half),
                                 start=True, stop=True).then_inc(qk_made, 1)

            def project_v(half, i, stages):
                mm_wait(f"v{half}", i, stages)
                width = HEAD_PAIRS * HEAD_DIM
                for n in range(PAIRS):
                    tokens = half_of(y1, half)[:, n * TOKENS:(n + 1) * TOKENS]
                    for e in range(2):
                        made = nc.tensor.matmul(mm_bank(f"v{half}")[64 * e:64 * e + 64,
                                                                    n * width:(n + 1) * width],
                                                tokens, wv[:, e, :, :], start=True, stop=True)
                made.then_inc(v_made, 1)

            def scores(unit, slot, j):
                pair = PAIRS * unit + j
                if j % HALF_PAIRS == 0:
                    half = j // HALF_PAIRS
                    pe.wait_ge(qk_ready, 4 * unit + 2 * half + 1)
                    pe.wait_ge(key_block_v, 2 * unit + half + 1)
                    pe.wait_ge(key_block_p, 2 * unit + half + 1)
                wait(pe, scores_shifted, pair)
                for n in range(2):
                    w = 2 * j + n
                    made = nc.tensor.matmul(score_bank[64 * n:64 * n + 64, 0:HEADS * TOKENS],
                                            q[:, slot, w * TOKENS:(w + 1) * TOKENS],
                                            k_block[:, slot, w, :, :], start=True, stop=True)
                made.then_inc(scores_made, 1)

            def turn_probs(unit, j):
                pair = PAIRS * unit + j
                pe.wait_ge(probs_ready, pair + 1)
                wait(pe, probs_t_ready, pair)
                for p in range(HEAD_PAIRS):
                    made = nc.tensor.transpose(probs_t_bank[:, p * 128:(p + 1) * 128],
                                               probs[:, j % 4, 2 * p:2 * p + 2, :], ident_sb[:, :])
                made.then_inc(probs_turned, 1)

            def times_v(unit, slot, j):
                pair = PAIRS * unit + j
                half = j // HALF_PAIRS
                if j % HALF_PAIRS == 0:
                    pe.wait_ge(v_ready, 2 * unit + half + 1)
                    wait(pe, attended_ready, 2 * unit + half)
                pe.wait_ge(probs_t_ready, pair + 1)
                for n in range(2):
                    for p in range(HEAD_PAIRS):
                        first = (j % HALF_PAIRS) * 128 + n * 64
                        made = nc.tensor.matmul(
                            pv_bank[32 * p:32 * p + 32, first:first + 64],
                            v_block[:, slot, 2 * j + n, p, :],
                            probs_t[:, half, p, j % HALF_PAIRS, n * 64:(n + 1) * 64],
                            start=True, stop=True)
                made.then_inc(pv_made, 1)
                if j % HALF_PAIRS == HALF_PAIRS - 1:
                    wait(pe, log_sum_made, 2 * unit + half)
                    for p in range(HEAD_PAIRS):
                        made = nc.tensor.matmul(sum_bank[32 * p:32 * p + 32, :], ones_pair_sb[:, :],
                                                probs_t[:, half, p, :, :], start=True, stop=True)
                    made.then_inc(sums_made, 1)

            def project(unit, half, i, stages):
                pe.wait_ge(attended_ready, 2 * unit + half + 1)
                mm_wait(f"proj{half}", i, stages)
                nc.tensor.matmul(mm_bank(f"proj{half}")[0:DIM, :], wproj[:, :], half_of(attended, half),
                                 start=True, stop=True).then_inc(proj_made, 1)

            def mlp_up(unit, half, i, stages):
                pe.wait_ge(y_ready[1], 2 * unit + half + 1)
                for chunk in range(HID_CHUNKS):
                    name = f"mlp1_{half * HID_CHUNKS + chunk}"
                    mm_wait(name, i, stages)
                    nc.tensor.matmul(mm_bank(name)[:, :], w1[:, chunk * 128:(chunk + 1) * 128],
                                     half_of(y2, half), start=True, stop=True).then_inc(mlp1_made, 1)

            def mlp_down(unit, half, i, stages):
                pe.wait_ge(gelu_ready, 2 * HID_CHUNKS * unit + HID_CHUNKS * (half + 1))
                name = f"mlp2_{half}"
                mm_wait(name, i, stages)
                for chunk in range(HID_CHUNKS):
                    made = nc.tensor.matmul(mm_bank(name)[0:DIM, :], w2[:, chunk, :],
                                            half_of(hidden[:, chunk, :], half),
                                            start=(chunk == 0), stop=(chunk == HID_CHUNKS - 1))
                made.then_inc(mlp2_made, 1)

            def denominators(unit, half, i, stages):
                pe.wait_ge(sq_ready, 2 * unit + half + 1)
                mm_wait(f"den{half}", i, stages)
                nc.tensor.matmul(mm_bank(f"den{half}")[0:DIM, :], wgdn[:, :], half_of(x3_sq, half),
                                 start=True, stop=True).then_inc(den_made, 1)

            def body(i, parity, stages):
                load, attend, finish, settle = (stage in stages for stage in UNIT_OF)
                other = 1 - parity
                def bank_after_load(half):
                    if isinstance(i, int) and i == UNITS:
                        return (y_ready[1], 2 * i - 4 + half + 1)
                    return (y_ready[0], 2 * i + half + 1)
                def bank_after_finish(half):
                    return (y_ready[1], 2 * i - 2 + half + 1) if finish else bank_after_load(half)
                for j in range(PAIRS):
                    if attend:
                        scores(i, parity, j)
                    draining = j < LAG
                    busy = finish if draining else attend
                    unit, slot = (i - 1, other) if draining else (i, parity)
                    at = (j - LAG) % PAIRS
                    if busy:
                        turn_probs(unit, at)
                    if finish and j == 0:
                        project(i - 1, 0, i, stages)
                    if finish and j == 1:
                        turn_in(1, i - 1, other, 0, bank_after_load(0))
                    if finish and j == 2:
                        turn_out(1, i - 1, 0)
                    if finish and j == 4:
                        mlp_up(i - 1, 0, i, stages)
                    if finish and j == 5:
                        mlp_up(i - 1, 1, i, stages)
                    if load and j == 6:
                        turn_out(0, i + 1, 1)
                    if load and j == 7:
                        project_qk("q1", wq, i + 1, 1, i, stages)
                    if busy:
                        times_v(unit, slot, at)
                    if j < 2:
                        if attend:
                            project_v(j, i, stages)
                        if settle:
                            mlp_down(i - 2, j, i, stages)
                    if j == 2:
                        if finish:
                            project(i - 1, 1, i, stages)
                        if settle:
                            denominators(i - 2, 0, i, stages)
                    if j == 3:
                        if finish:
                            turn_in(1, i - 1, other, 1, bank_after_load(1))
                        if settle:
                            denominators(i - 2, 1, i, stages)
                        if load:
                            turn_in(0, i + 1, other, 0, bank_after_finish(0))
                    if j == 4:
                        if finish:
                            turn_out(1, i - 1, 1)
                        if load:
                            turn_in(0, i + 1, other, 1, bank_after_finish(1))
                    if load and j == 5:
                        turn_out(0, i + 1, 0)
                    if load and j == 6:
                        project_qk("q0", wq, i + 1, 0, i, stages)
                        project_qk("k0", wk, i + 1, 0, i, stages)
                    if load and j == 7:
                        project_qk("k1", wk, i + 1, 1, i, stages)

            iterations(pe, body)


def kernel(x, L0_conv_norm1_w, L0_conv_norm1_b, L0_conv_qkv_w, L0_conv_qkv_b, L0_conv_proj_w,
           L0_conv_proj_b, L0_conv_norm2_w, L0_conv_norm2_b, L0_conv_mlp_w1, L0_conv_mlp_b1,
           L0_conv_mlp_w2, L0_conv_mlp_b2, L1_conv_beta, L1_conv_gamma):
    import numpy as np
    import concourse.bacc as bacc
    from concourse.bass_utils import run_bass_kernel_spmd

    low, right = (np.arange(TOKENS) // WIN >= SHIFT).astype(int), (np.arange(TOKENS) % WIN >= SHIFT).astype(int)
    quadrant = 2 * low + right
    is_in = (quadrant[None, :] == np.arange(4)[:, None]).astype(np.float32)
    qmask = np.zeros((ROWS, MASK_ROWS, WINDOWS, TOKENS), np.float32)
    qmask[:ROWS - 1, 0:4] = is_in[None, :, None, :]
    qmask[ROWS - 1, 4:8] = is_in[:, None, :]
    side_differs = (np.arange(4)[:, None] % 2 != right[None, :])
    height_differs = (np.arange(4)[:, None] // 2 != low[None, :])
    kmask = np.zeros((MASK_ROWS, WINDOWS, HEADS, TOKENS), np.float32)
    kmask[0:4, WINDOWS - 1] = np.where(side_differs, MASKED, 0.0)[:, None, :]
    kmask[4:8, :WINDOWS - 1] = np.where(height_differs, MASKED, 0.0)[:, None, None, :]
    kmask[4:8, WINDOWS - 1] = np.where(side_differs | height_differs, MASKED, 0.0)[:, None, :]
    head_mask = (np.arange(DIM)[:, None] // HEAD_DIM == np.arange(HEADS)[None, :]).astype(np.float32)
    ones_pair = (np.arange(128)[:, None] // 64 == np.arange(32)[None, :] // HEAD_DIM).astype(np.float32)

    col, row = (-1, 1), (1, -1)
    arrays = {
        "x": x, "qmask": qmask.reshape(ROWS, MASK_ROWS, UNIT), "kmask": kmask.reshape(MASK_ROWS, -1),
        "ident": np.eye(128, dtype=np.float32), "head_mask": head_mask, "ones_pair": ones_pair,
        "norm1_w": np.reshape(L0_conv_norm1_w, col), "norm1_b": np.reshape(L0_conv_norm1_b, col),
        "qkv_t": np.transpose(L0_conv_qkv_w), "qkv_b": np.reshape(L0_conv_qkv_b, row),
        "proj_t": np.transpose(L0_conv_proj_w), "proj_b": np.reshape(L0_conv_proj_b, row),
        "norm2_w": np.reshape(L0_conv_norm2_w, col), "norm2_b": np.reshape(L0_conv_norm2_b, col),
        "w1_t": np.transpose(L0_conv_mlp_w1), "b1": np.reshape(L0_conv_mlp_b1, row),
        "w2_t": np.transpose(L0_conv_mlp_w2), "b2": np.reshape(L0_conv_mlp_b2, col),
        "beta": np.reshape(L1_conv_beta, row), "gamma_t": np.transpose(L1_conv_gamma),
    }
    nc = bacc.Bacc("TRN2", target_bir_lowering=False, num_devices=1)
    sent, aps = {}, {}
    for name, a in arrays.items():
        a = np.ascontiguousarray(a)
        sent[f"in_{name}"] = a
        aps[name] = nc.dram_tensor(f"in_{name}", a.shape, mybir.dt.from_np(a.dtype),
                                   kind="ExternalInput").ap()
    out = nc.dram_tensor("out_0", (N_IMAGES, DIM, HEIGHT, WIDTH), mybir.dt.float32,
                         kind="ExternalOutput").ap()
    window_block(nc, out=out, **aps)
    result = run_bass_kernel_spmd(nc, [sent], core_ids=[0])
    return result.results[0]["out_0"]
```

```python
import concourse.bass as bass
from concourse import mybir
from contextlib import ExitStack

N_IMAGES, DIM, HEIGHT, WIDTH = 4, 96, 128, 128
HEADS, WIN, SHIFT = 6, 8, 4
HEAD_DIM = DIM // HEADS
HIDDEN = 4 * DIM
HID_CHUNKS = HIDDEN // 128
ROWS = HEIGHT // WIN
WINDOWS = WIDTH // WIN
TOKENS = WIN * WIN
UNIT = WINDOWS * TOKENS
UNITS = N_IMAGES * ROWS
HALF = UNIT // 2
HALVES = 2 * UNITS
HALF_WINDOWS = WINDOWS // 2
PAIRS = HALF_WINDOWS // 2
HEAD_PAIRS = HEADS // 2
CHUNKS = HALF // 128
MASK_ROWS = 8
LN_EPS = 1e-5
PEDESTAL = 2.0 ** -36
BOUND_BETA = (1e-6 + PEDESTAL) ** 0.5
BOUND_GAMMA = PEDESTAL ** 0.5
MASKED = -100.0
X_SLOTS = 4
TURN_IN, TURN_OUT, QK, ATTEND, PROJECT, MLP, SETTLE = 4, 3, 1, 0, -1, -2, -3


def window_block(nc, x, qmask, kmask, ident, head_mask, ones_pair, norm1_w, norm1_b, qkv_t, qkv_b,
                 proj_t, proj_b, norm2_w, norm2_b, w1_t, b1, w2_t, b2, beta, gamma_t, out):
    f32 = mybir.dt.float32
    ALU = mybir.AluOpType
    ACT = mybir.ActivationFunctionType
    AX = mybir.AxisListType

    ctx = ExitStack()
    with ctx:
        def sb(name, shape, dt=f32):
            return ctx.enter_context(nc.sbuf_tensor(name, shape, dt))

        def bank(name):
            return ctx.enter_context(nc.psum_tensor(name, [128, 512], f32))

        def sem(name):
            return ctx.enter_context(nc.semaphore(name))

        ident_sb = sb("ident_sb", [128, 128])
        head_mask_sb = sb("head_mask_sb", [DIM, HEADS])
        ones_pair_sb = sb("ones_pair_sb", [128, 32])
        qkv_raw = sb("qkv_raw", [DIM, 3 * DIM])
        w1_raw = sb("w1_raw", [DIM, HIDDEN])
        norm_cols = sb("norm_cols", [DIM, 4])
        b2_col = sb("b2_col", [DIM, 1])
        wq = sb("wq", [DIM + 1, DIM])
        wk = sb("wk", [DIM + 1, DIM])
        wv = sb("wv", [128, 2, HEAD_PAIRS, HEAD_DIM])
        wproj = sb("wproj", [DIM + 1, DIM])
        w1 = sb("w1", [DIM + 1, HIDDEN])
        w2 = sb("w2", [128, HID_CHUNKS, DIM])
        wgdn = sb("wgdn", [DIM + 1, DIM])
        gdn_raw = sb("gdn_raw", [DIM + 1, DIM])
        qkv_bias = sb("qkv_bias", [DIM + 1, 3 * DIM])
        b1_row = sb("b1_row", [DIM + 1, HIDDEN])
        eps_col = sb("eps_col", [128, 1])

        x_ext = sb("x_ext", [DIM, X_SLOTS, WIN, WIDTH + SHIFT])
        o_ext = sb("o_ext", [DIM, 2, WIN, WIDTH + SHIFT])
        stats = [sb(f"stats{n}", [128, 2 * CHUNKS, 6]) for n in (1, 2)]
        moments = [sb(f"moments{n}", [128, 2 * CHUNKS, 2]) for n in (1, 2)]
        log_var = [sb(f"log_var{n}", [128, 2 * CHUNKS]) for n in (1, 2)]
        rstd = [sb(f"rstd{n}", [128, 2 * CHUNKS]) for n in (1, 2)]
        y_tok = [sb(f"y_tok{n}", [128, 2 * CHUNKS, DIM]) for n in (1, 2)]
        y1 = sb("y1", [128, 2, UNIT])
        y2 = sb("y2", [DIM + 1, UNIT])
        q = sb("q", [128, 2, UNIT])
        k = sb("k", [DIM, UNIT])
        k_block = sb("k_block", [128, WINDOWS, HEADS, TOKENS])
        v_block = sb("v_block", [128, WINDOWS, HEAD_PAIRS, 32])
        row_max = sb("row_max", [128, 2, HEADS])
        shifted = sb("shifted", [128, 2, HEADS, TOKENS])
        probs = sb("probs", [128, 4, HEADS, TOKENS])
        probs_t = sb("probs_t", [128, 2, HEAD_PAIRS, PAIRS, 128])
        log_sum = sb("log_sum", [DIM, HALF])
        inv_sum = sb("inv_sum", [DIM, HALF])
        attended = sb("attended", [DIM + 1, UNIT])
        x2 = sb("x2", [DIM, 2, UNIT])
        hidden = sb("hidden", [128, HID_CHUNKS, UNIT])
        x3 = sb("x3", [DIM, UNIT])
        x3_sq = sb("x3_sq", [DIM + 1, UNIT])
        log_den = sb("log_den", [DIM, UNIT])
        inv_den = sb("inv_den", [DIM, UNIT])

        score_bank = bank("score_bank")
        probs_t_bank = bank("probs_t_bank")
        pv_bank = bank("pv_bank")
        sum_bank = bank("sum_bank")
        turn_banks = [bank("turn_bank1"), bank("turn_bank2")]
        mm_banks = [bank("mm_bank0"), bank("mm_bank1")]

        waits_passed = sem("waits_passed")
        consts_loaded = sem("consts_loaded")
        key_mask_loaded = sem("key_mask_loaded")
        cleared = sem("cleared")
        pads_cleared = sem("pads_cleared")
        weights_folded = sem("weights_folded")
        bias_products = sem("bias_products")
        x_loaded = [sem(f"x_loaded{n}") for n in range(X_SLOTS)]
        query_mask_loaded = [sem("query_mask_loaded0"), sem("query_mask_loaded1")]
        out_stored = [sem("out_stored0"), sem("out_stored1")]
        x_wrapped = sem("x_wrapped")
        out_wrapped = sem("out_wrapped")
        x_turned = [sem("x_turned1"), sem("x_turned2")]
        stats_made = [sem("stats_made1"), sem("stats_made2")]
        moments_ready = [sem("moments_ready1"), sem("moments_ready2")]
        log_var_made = [sem("log_var_made1"), sem("log_var_made2")]
        rstd_ready = [sem("rstd_ready1"), sem("rstd_ready2")]
        normed = [sem("normed1"), sem("normed2")]
        y_turned = [sem("y_turned1"), sem("y_turned2")]
        y_ready = [sem("y_ready1"), sem("y_ready2")]
        q_made = sem("q_made")
        k_made = sem("k_made")
        q_ready = sem("q_ready")
        k_ready = sem("k_ready")
        key_block_v = sem("key_block_v")
        key_block_p = sem("key_block_p")
        v_made = sem("v_made")
        v_ready = sem("v_ready")
        scores_made = sem("scores_made")
        max_ready = sem("max_ready")
        scores_shifted = sem("scores_shifted")
        probs_ready = sem("probs_ready")
        probs_turned = sem("probs_turned")
        probs_t_ready = sem("probs_t_ready")
        pv_made = sem("pv_made")
        sums_made = sem("sums_made")
        log_sum_made = sem("log_sum_made")
        inv_sum_ready = sem("inv_sum_ready")
        attended_ready = sem("attended_ready")
        proj_made = sem("proj_made")
        x2_ready = sem("x2_ready")
        mlp1_made = sem("mlp1_made")
        gelu_ready = sem("gelu_ready")
        mlp2_made = sem("mlp2_made")
        x3_ready = sem("x3_ready")
        sq_ready = sem("sq_ready")
        den_made = sem("den_made")
        log_den_made = sem("log_den_made")
        inv_den_ready = sem("inv_den_ready")
        out_ready = sem("out_ready")

        def iterations(engine, body):
            first = 2
            trips = (UNITS - 2 - first) // X_SLOTS
            for i in range(-2, first):
                body(i, i % X_SLOTS)
            with engine.Fori(0, trips) as trip:
                for n in range(X_SLOTS):
                    body(X_SLOTS * trip + (first + n), (first + n) % X_SLOTS)
            for i in range(first + X_SLOTS * trips, UNITS + 2):
                body(i, i % X_SLOTS)

        def rounds(engine, steps):
            def body(i, m):
                for n in range(2):
                    H, h = 2 * i + n, 2 * m + n
                    def run(stage, offset, *rest):
                        if has(H + offset):
                            stage(H + offset, (h + offset) % (2 * X_SLOTS), *rest)
                    steps(run)
            iterations(engine, body)

        def has(at, count=HALVES):
            return not isinstance(at, int) or 0 <= at < count

        def wait(engine, semaphore, count):
            if not isinstance(count, int) or count > 0:
                engine.wait_ge(semaphore, count)

        def wait_alone(engine, semaphore, count):
            engine.wait_ge(semaphore, count)
            engine.sem_inc(waits_passed, 1)

        MM_ITEMS = [
            ("v", ATTEND, v_ready, 1, 1), ("q", QK, q_ready, 1, 1), ("mlp2", SETTLE, x3_ready, 1, 1),
            ("k", QK, k_ready, 1, 1), ("den", SETTLE, log_den_made, 1, 1), ("proj", PROJECT, x2_ready, 1, 1),
            *((f"mlp1_{n}", MLP, gelu_ready, HID_CHUNKS, n + 1) for n in range(HID_CHUNKS)),
        ]
        MM_AT = {item[0]: at for at, item in enumerate(MM_ITEMS)}
        def mm_bank(name, a):
            h = a - MM_ITEMS[MM_AT[name]][1]
            return mm_banks[(MM_AT[name] + len(MM_ITEMS) * h) % 2]

        def mm_bank_emptied(name, A):
            at, H = MM_AT[name], A - MM_ITEMS[MM_AT[name]][1]
            for back in range(1, 100):
                other = at - 2 * back
                _, offset, semaphore, per_half, own = MM_ITEMS[other % len(MM_ITEMS)]
                B = H + other // len(MM_ITEMS) + offset
                if has(B):
                    return semaphore, per_half * B + own
            return None

        def windows_of(tile, a):
            first = SHIFT + (a % 2) * (WIDTH // 2)
            return tile[:, :, first:first + WIDTH // 2].rearrange("c r (n w) -> c n r w", w=WIN)

        def in_windows(flat):
            return flat.rearrange("c (n r w) -> c n r w", r=WIN, w=WIN)

        def half_of(tile, a):
            return tile[:, (a % 2) * HALF:(a % 2 + 1) * HALF]

        def unit_slot(a, slots=2):
            return (a // 2) % slots

        def chunks_of(a):
            return range((a % 2) * CHUNKS, (a % 2 + 1) * CHUNKS)

        def half_windows(a):
            return slice((a % 2) * HALF_WINDOWS, (a % 2 + 1) * HALF_WINDOWS)

        block = ctx.enter_context(nc.Block())

        @block.sync
        def _(sp):
            for dst, src in ((ident_sb[:, :], ident), (head_mask_sb[:, :], head_mask),
                             (ones_pair_sb[:, :], ones_pair), (qkv_raw[:, :], qkv_t),
                             (w1_raw[:, :], w1_t), (norm_cols[:, 0:1], norm1_w),
                             (norm_cols[:, 1:2], norm1_b), (norm_cols[:, 2:3], norm2_w),
                             (norm_cols[:, 3:4], norm2_b), (b2_col[:, :], b2),
                             (wproj[0:DIM, :], proj_t), (wproj[DIM:DIM + 1, :], proj_b),
                             (w2[:, :, :], w2_t.rearrange("(c p) n -> p c n", p=128)),
                             (gdn_raw[0:DIM, :], gamma_t), (gdn_raw[DIM:DIM + 1, :], beta),
                             (qkv_bias[DIM:DIM + 1, :], qkv_b), (b1_row[DIM:DIM + 1, :], b1)):
                sp.dma_start(dst, src).then_inc(consts_loaded, 16)

            def image_rows(unit):
                row = unit % ROWS
                return (0, row * WIN + SHIFT), (SHIFT, ((row + 1) % ROWS) * WIN)

            def load_x(unit, slot):
                for at, first in image_rows(unit):
                    sp.dma_start(x_ext[:, slot, at:at + SHIFT, 0:WIDTH],
                                 x[bass.ds(unit // ROWS, 1), :, bass.ds(first, SHIFT), :]
                                 .rearrange("n c h w -> (n c) h w")).then_inc(x_loaded[slot], 16)

            def load_query_mask(unit, slot):
                sp.dma_start(q[DIM:DIM + MASK_ROWS, slot, :],
                             qmask[bass.ds(unit % ROWS, 1), :, :].rearrange("n m t -> (n m) t"))\
                    .then_inc(query_mask_loaded[slot], 16)

            def store_out(unit, slot):
                for at, first in image_rows(unit):
                    sp.dma_start(out[bass.ds(unit // ROWS, 1), :, bass.ds(first, SHIFT), :]
                                 .rearrange("n c h w -> (n c) h w"),
                                 o_ext[:, slot, at:at + SHIFT, 0:WIDTH])\
                        .then_inc(out_stored[slot], 16)

            def body(i, m):
                if has(i + 2, UNITS):
                    if has(i - 2, UNITS):
                        wait_alone(sp, x2_ready, 2 * (i - 1))
                    load_x(i + 2, (m + 2) % X_SLOTS)
                if has(i + 1, UNITS):
                    if has(i - 1, UNITS):
                        wait_alone(sp, scores_made, 2 * PAIRS * i)
                    elif i == -1:
                        sp.wait_ge(pads_cleared, 1)
                    load_query_mask(i + 1, (m + 1) % 2)
                if has(i - 2, UNITS):
                    wait_alone(sp, out_wrapped, i - 1)
                    store_out(i - 2, m % 2)

            iterations(sp, body)
            for slot in range(2):
                sp.wait_ge(out_stored[slot], 32 * (UNITS // 2))

        @block.gpsimd
        def _(pool):
            nc.gpsimd.memset(q[DIM:128, :, :], 0.0).then_inc(pads_cleared, 1)
            nc.gpsimd.memset(k_block[DIM:128, :, :, :], 0.0).then_inc(pads_cleared, 1)
            pool.wait_ge(pads_cleared, 2)
            pool.dma_start(k_block[DIM:DIM + MASK_ROWS, :, :, :].rearrange("m n h t -> m (n h t)"),
                           kmask).then_inc(key_mask_loaded, 16)
            pool.wait_ge(consts_loaded, 16 * 17)

            def wrap_x(unit, slot):
                wait_alone(pool, x_loaded[slot], 32 * (unit // X_SLOTS + 1))
                nc.gpsimd.tensor_copy(x_ext[:, slot, :, WIDTH:WIDTH + SHIFT],
                                      x_ext[:, slot, :, 0:SHIFT]).then_inc(x_wrapped, 2)

            def key_blocks(A, a):
                wait_alone(pool, k_ready, A + 1)
                for h in range(HEADS // 2):
                    made = nc.gpsimd.tensor_scalar(
                        k_block[0:DIM, half_windows(a), h, :],
                        half_of(k, a).rearrange("c (n t) -> c n t", t=TOKENS),
                        head_mask_sb[:, h:h + 1], 1.0, ALU.mult, ALU.mult)
                made.then_inc(key_block_p, 1)

            def wrap_out(unit, slot):
                wait_alone(pool, out_ready, 2 * (unit + 1))
                nc.gpsimd.tensor_copy(o_ext[:, slot, :, 0:SHIFT],
                                      o_ext[:, slot, :, WIDTH:WIDTH + SHIFT]).then_inc(out_wrapped, 1)

            def body(i, m):
                if has(i + 2, UNITS):
                    wrap_x(i + 2, (m + 2) % X_SLOTS)
                if has(2 * i + QK):
                    key_blocks(2 * i + QK, QK)
                if has(i - 2, UNITS):
                    wrap_out(i - 2, m % 2)
                if has(2 * i + 1 + QK):
                    key_blocks(2 * i + 1 + QK, 1 + QK)

            iterations(pool, body)

        @block.scalar
        def _(act):
            def rstd_of(A, a, ln):
                act.wait_ge(moments_ready[ln], A + 1)
                cols = slice(chunks_of(a)[0], chunks_of(a)[-1] + 1)
                nc.scalar.activation(log_var[ln][:, cols], moments[ln][:, cols, 1], ACT.Ln,
                                     bias=eps_col[:, :]).then_inc(log_var_made[ln], 1)
                act.wait_ge(log_var_made[ln], A + 1)
                nc.scalar.activation(rstd[ln][:, cols], log_var[ln][:, cols], ACT.Exp, scale=-0.5)\
                    .then_inc(rstd_ready[ln], 1)

            def y_copy(A, a, ln):
                act.wait_ge(y_turned[ln], A + 1)
                if ln == 0:
                    rows = slice(chunks_of(a)[0], chunks_of(a)[-1] + 1)
                    dst = in_windows(y1[0:DIM, unit_slot(a), :])[:, :, rows, :]
                    src = turn_banks[ln][0:DIM, :].rearrange("c (r n w) -> c n r w", r=CHUNKS, w=WIN)
                else:
                    dst, src = half_of(y2[0:DIM, :], a), turn_banks[ln][0:DIM, :]
                nc.scalar.activation(dst, src, ACT.Copy).then_inc(y_ready[ln], 1)

            def q_copy(A, a):
                act.wait_ge(q_made, A + 1)
                nc.scalar.activation(half_of(q[0:DIM, unit_slot(a), :], a), mm_bank("q", a)[0:DIM, :],
                                     ACT.Copy).then_inc(q_ready, 1)

            def k_copy(A, a):
                act.wait_ge(k_made, A + 1)
                wait(act, key_block_v, A - 1)
                wait(act, key_block_p, A - 1)
                nc.scalar.activation(half_of(k, a), mm_bank("k", a)[0:DIM, :], ACT.Copy)\
                    .then_inc(k_ready, 1)

            def softmax_exp(A, a, p):
                pair = PAIRS * A + p
                act.wait_ge(scores_shifted, pair + 1)
                wait(act, probs_turned, pair - 3)
                nc.scalar.activation(probs[:, p, :, :], shifted[:, p % 2, :, :], ACT.Exp)\
                    .then_inc(probs_ready, 1)

            def probs_t_copy(A, a, p):
                act.wait_ge(probs_turned, PAIRS * A + p + 1)
                nc.scalar.activation(probs_t[:, a % 2, :, p, :],
                                     probs_t_bank[:, 0:HEAD_PAIRS * 128]
                                     .rearrange("k (p t) -> k p t", p=HEAD_PAIRS), ACT.Copy)\
                    .then_inc(probs_t_ready, 1)

            def inverse_sums(A, a):
                act.wait_ge(sums_made, A + 1)
                nc.scalar.activation(log_sum[:, :], sum_bank[0:DIM, :], ACT.Ln).then_inc(log_sum_made, 1)
                act.wait_ge(log_sum_made, A + 1)
                wait(act, attended_ready, A)
                nc.scalar.activation(inv_sum[:, :], log_sum[:, :], ACT.Exp, scale=-1.0)\
                    .then_inc(inv_sum_ready, 1)

            def gelus(A, a):
                for n in range(HID_CHUNKS):
                    act.wait_ge(mlp1_made, HID_CHUNKS * A + n + 1)
                    nc.scalar.activation(half_of(hidden[:, n, :], a), mm_bank(f"mlp1_{n}", a)[:, :],
                                         ACT.Gelu).then_inc(gelu_ready, 1)

            def squares(A, a):
                act.wait_ge(x3_ready, A + 1)
                nc.scalar.activation(half_of(x3_sq[0:DIM, :], a), half_of(x3, a), ACT.Square)\
                    .then_inc(sq_ready, 1)

            def inverse_denominators(A, a):
                act.wait_ge(den_made, A + 1)
                nc.scalar.activation(half_of(log_den, a), mm_bank("den", a)[0:DIM, :], ACT.Ln)\
                    .then_inc(log_den_made, 1)
                act.wait_ge(log_den_made, A + 1)
                nc.scalar.activation(half_of(inv_den, a), half_of(log_den, a), ACT.Exp, scale=-0.5)\
                    .then_inc(inv_den_ready, 1)

            def steps(run):
                nc.scalar.preload_act_table_set("natural_log_exp_and_others")
                run(probs_t_copy, ATTEND - 1, 2)
                run(softmax_exp, ATTEND - 1, 3)
                run(softmax_exp, ATTEND, 0)
                run(rstd_of, TURN_OUT, 0)
                run(rstd_of, MLP, 1)
                run(q_copy, QK)
                run(probs_t_copy, ATTEND - 1, 3)
                run(softmax_exp, ATTEND, 1)
                run(inverse_sums, PROJECT)
                run(y_copy, TURN_OUT, 0)
                run(squares, SETTLE)
                run(probs_t_copy, ATTEND, 0)
                run(softmax_exp, ATTEND, 2)
                run(y_copy, MLP, 1)
                run(k_copy, QK)
                run(inverse_denominators, SETTLE)
                nc.scalar.preload_act_table_set("gelu_and_others")
                run(probs_t_copy, ATTEND, 1)
                run(gelus, MLP)

            rounds(act, steps)

        @block.vector
        def _(dve):
            nc.vector.memset(y1[DIM:128, :, :], 0.0).then_inc(cleared, 1)
            nc.vector.memset(wv[DIM:128, :, :, :], 0.0).then_inc(cleared, 1)
            nc.vector.memset(v_block[:, :, :, :], 0.0).then_inc(cleared, 1)
            nc.vector.memset(y2[DIM:DIM + 1, :], 1.0).then_inc(cleared, 1)
            nc.vector.memset(attended[DIM:DIM + 1, :], 1.0).then_inc(cleared, 1)
            nc.vector.memset(x3_sq[DIM:DIM + 1, :], 1.0).then_inc(cleared, 1)
            nc.vector.memset(eps_col[:, :], LN_EPS).then_inc(cleared, 1)
            dve.wait_ge(cleared, 7)
            nc.vector.memset(y1[DIM:DIM + 1, :, :], 1.0).then_inc(cleared, 1)
            dve.wait_ge(consts_loaded, 16 * 17)
            head_scale = HEAD_DIM ** -0.5
            nc.vector.tensor_scalar(wq[0:DIM, :], qkv_raw[:, 0:DIM], norm_cols[:, 0:1], head_scale,
                                    ALU.mult, ALU.mult)
            nc.vector.tensor_scalar(wk[0:DIM, :], qkv_raw[:, DIM:2 * DIM], norm_cols[:, 0:1], None,
                                    ALU.mult)
            def even_odd(row):
                return row.rearrange("c (p e d) -> c e p d", e=2, d=HEAD_DIM)
            nc.vector.tensor_scalar(wv[0:DIM, :, :, :], even_odd(qkv_raw[:, 2 * DIM:3 * DIM]),
                                    norm_cols[:, 0:1], None, ALU.mult)
            nc.vector.tensor_scalar(w1[0:DIM, :], w1_raw[:, :], norm_cols[:, 2:3], None, ALU.mult)
            nc.vector.tensor_scalar(gdn_raw[0:DIM, :], gdn_raw[0:DIM, :], BOUND_GAMMA, None, ALU.max)\
                .then_inc(weights_folded, 1)
            nc.vector.tensor_scalar(gdn_raw[DIM:DIM + 1, :], gdn_raw[DIM:DIM + 1, :], BOUND_BETA, None,
                                    ALU.max).then_inc(weights_folded, 1)
            dve.wait_ge(weights_folded, 2)
            nc.vector.tensor_tensor(wgdn[:, :], gdn_raw[:, :], gdn_raw[:, :], ALU.mult)\
                .then_inc(weights_folded, 1)
            dve.wait_ge(weights_folded, 3)
            nc.vector.tensor_scalar(wgdn[:, :], wgdn[:, :], -PEDESTAL, None, ALU.add)
            dve.wait_ge(bias_products, 1)
            row = slice(DIM, DIM + 1)
            qkv_shift = score_bank[row, 0:3 * DIM]
            nc.vector.tensor_tensor(qkv_bias[row, :], qkv_shift, qkv_bias[row, :], ALU.add)\
                .then_inc(weights_folded, 1)
            nc.vector.tensor_tensor(w1[row, :], pv_bank[row, 0:HIDDEN], b1_row[row, :], ALU.add)
            dve.wait_ge(weights_folded, 4)
            nc.vector.tensor_scalar(wq[row, :], qkv_bias[row, 0:DIM], head_scale, None, ALU.mult)
            nc.vector.tensor_copy(wk[row, :], qkv_bias[row, DIM:2 * DIM])
            nc.vector.tensor_copy(wv[row, :, :, :], even_odd(qkv_bias[row, 2 * DIM:3 * DIM]))\
                .then_inc(weights_folded, 1)

            def statistics(A, a, ln):
                dve.wait_ge(x_turned[ln], A + 1)
                for n, c in enumerate(chunks_of(a)):
                    made = nc.vector.bn_stats(stats[ln][:, c, :],
                                              turn_banks[ln][:, n * DIM:(n + 1) * DIM])
                made.then_inc(stats_made[ln], 1)
                wait_alone(dve, stats_made[ln], A + 1)
                for c in chunks_of(a):
                    made = nc.vector.bn_aggr(moments[ln][:, c, :], stats[ln][:, c, :])
                made.then_inc(moments_ready[ln], 1)

            def normalise(A, a, ln):
                dve.wait_ge(rstd_ready[ln], A + 1)
                for n, c in enumerate(chunks_of(a)):
                    made = nc.vector.tensor_scalar(y_tok[ln][:, c, :],
                                                   turn_banks[ln][:, n * DIM:(n + 1) * DIM],
                                                   moments[ln][:, c, 0:1], rstd[ln][:, c:c + 1],
                                                   ALU.subtract, ALU.mult)
                made.then_inc(normed[ln], 1)

            def key_blocks(A, a):
                dve.wait_ge(k_ready, A + 1)
                for h in range(HEADS // 2, HEADS):
                    made = nc.vector.tensor_scalar(
                        k_block[0:DIM, half_windows(a), h, :],
                        half_of(k, a).rearrange("c (n t) -> c n t", t=TOKENS),
                        head_mask_sb[:, h:h + 1], None, ALU.mult)
                made.then_inc(key_block_v, 1)

            def v_blocks(A, a):
                dve.wait_ge(v_made, A + 1)
                for e in range(2):
                    rows = slice(64 * e, 64 * e + 64)
                    made = nc.vector.tensor_copy(
                        v_block[rows, half_windows(a), :, HEAD_DIM * e:HEAD_DIM * (e + 1)],
                        mm_bank("v", a)[rows, 0:HALF_WINDOWS * HEAD_PAIRS * HEAD_DIM]
                        .rearrange("k (n p d) -> k n p d", n=HALF_WINDOWS, p=HEAD_PAIRS))
                made.then_inc(v_ready, 1)

            def shift_scores(A, a, p):
                pair = PAIRS * A + p
                dve.wait_ge(scores_made, pair + 1)
                scores = score_bank[:, 0:HEADS * TOKENS].rearrange("t (h k) -> t h k", h=HEADS)
                nc.vector.tensor_reduce(row_max[:, p % 2, :], scores, op=ALU.max, axis=AX.X)\
                    .then_inc(max_ready, 1)
                dve.wait_ge(max_ready, pair + 1)
                wait(dve, probs_ready, pair - 1)
                nc.vector.tensor_tensor(shifted[:, p % 2, :, :], scores,
                                        row_max[:, p % 2, :].unsqueeze(2)
                                        .broadcast_to([128, HEADS, TOKENS]), ALU.subtract)\
                    .then_inc(scores_shifted, 1)

            def divide(A, a):
                dve.wait_ge(inv_sum_ready, A + 1)
                dve.wait_ge(pv_made, PAIRS * (A + 1))
                nc.vector.tensor_tensor(half_of(attended[0:DIM, :], a), pv_bank[0:DIM, :],
                                        inv_sum[:, :], ALU.mult).then_inc(attended_ready, 1)

            def first_residual(A, a):
                dve.wait_ge(proj_made, A + 1)
                nc.vector.tensor_tensor(in_windows(half_of(x2[:, unit_slot(a), :], a)),
                                        in_windows(mm_bank("proj", a)[0:DIM, :]),
                                        windows_of(x_ext[:, unit_slot(a, X_SLOTS), :, :], a), ALU.add)\
                    .then_inc(x2_ready, 1)

            def second_residual(A, a):
                dve.wait_ge(mlp2_made, A + 1)
                nc.vector.scalar_tensor_tensor(half_of(x3, a), mm_bank("mlp2", a)[0:DIM, :],
                                               b2_col[:, :], half_of(x2[:, unit_slot(a), :], a),
                                               ALU.add, ALU.add).then_inc(x3_ready, 1)

            def outputs(A, a):
                dve.wait_ge(inv_den_ready, A + 1)
                wait(dve, out_stored[unit_slot(a)], 32 * (A // 4))
                nc.vector.tensor_tensor(windows_of(o_ext[:, unit_slot(a), :, :], a),
                                        in_windows(half_of(x3, a)), in_windows(half_of(inv_den, a)),
                                        ALU.mult).then_inc(out_ready, 1)

            def steps(run):
                run(shift_scores, ATTEND, 0)
                run(statistics, MLP, 1)
                run(v_blocks, ATTEND)
                run(normalise, TURN_OUT, 0)
                run(shift_scores, ATTEND, 1)
                run(normalise, MLP, 1)
                run(divide, PROJECT)
                run(second_residual, SETTLE)
                run(shift_scores, ATTEND, 2)
                run(first_residual, PROJECT)
                run(shift_scores, ATTEND, 3)
                run(statistics, TURN_IN, 0)
                run(key_blocks, QK)
                run(outputs, SETTLE)

            rounds(dve, steps)

        @block.tensor
        def _(pe):
            pe.wait_ge(consts_loaded, 16 * 17)
            row = slice(DIM, DIM + 1)
            nc.tensor.matmul(score_bank[row, 0:3 * DIM], norm_cols[:, 1:2], qkv_raw[:, :],
                             start=True, stop=True)
            nc.tensor.matmul(pv_bank[row, 0:HIDDEN], norm_cols[:, 3:4], w1_raw[:, :],
                             start=True, stop=True).then_inc(bias_products, 1)
            pe.wait_ge(weights_folded, 5)
            pe.wait_ge(cleared, 8)
            pe.wait_ge(pads_cleared, 2)
            pe.wait_ge(key_mask_loaded, 16)

            def mm_wait(name, A):
                found = mm_bank_emptied(name, A)
                if found is not None:
                    wait(pe, *found)

            def turn_in(A, a, ln):
                if ln == 0:
                    pe.wait_ge(x_wrapped, A + 1)
                else:
                    pe.wait_ge(x2_ready, A + 1)
                wait(pe, y_ready[ln], A)
                for n, c in enumerate(chunks_of(a)):
                    if ln == 0:
                        chunk = x_ext[:, unit_slot(a, X_SLOTS), c, SHIFT:SHIFT + WIDTH]
                    else:
                        chunk = x2[:, unit_slot(a), c * 128:(c + 1) * 128]
                    made = nc.tensor.transpose(turn_banks[ln][:, n * DIM:(n + 1) * DIM], chunk,
                                               ident_sb[0:DIM, 0:DIM])
                made.then_inc(x_turned[ln], 1)

            def turn_out(A, a, ln):
                pe.wait_ge(normed[ln], A + 1)
                for n, c in enumerate(chunks_of(a)):
                    made = nc.tensor.transpose(turn_banks[ln][0:DIM, n * 128:(n + 1) * 128],
                                               y_tok[ln][:, c, :], ident_sb[:, :])
                made.then_inc(y_turned[ln], 1)

            def project_q(A, a):
                pe.wait_ge(y_ready[0], A + 2 - a % 2)
                mm_wait("q", A)
                nc.tensor.matmul(mm_bank("q", a)[0:DIM, :], wq[:, :],
                                 half_of(y1[0:DIM + 1, unit_slot(a), :], a),
                                 start=True, stop=True).then_inc(q_made, 1)

            def project_k(A, a):
                mm_wait("k", A)
                nc.tensor.matmul(mm_bank("k", a)[0:DIM, :], wk[:, :],
                                 half_of(y1[0:DIM + 1, unit_slot(a), :], a),
                                 start=True, stop=True).then_inc(k_made, 1)

            def project_v(A, a):
                mm_wait("v", A)
                width = HEAD_PAIRS * HEAD_DIM
                for n in range(HALF_WINDOWS):
                    tokens = half_of(y1[:, unit_slot(a), :], a)[:, n * TOKENS:(n + 1) * TOKENS]
                    for e in range(2):
                        made = nc.tensor.matmul(mm_bank("v", a)[64 * e:64 * e + 64,
                                                             n * width:(n + 1) * width],
                                                tokens, wv[:, e, :, :], start=True, stop=True)
                made.then_inc(v_made, 1)

            def scores(A, a, p):
                if p == 0:
                    pe.wait_ge(q_ready, A + 1)
                    pe.wait_ge(query_mask_loaded[unit_slot(a)], 16 * (A // 4 + 1))
                    pe.wait_ge(key_block_v, A + 1)
                    pe.wait_ge(key_block_p, A + 1)
                wait(pe, scores_shifted, PAIRS * A + p)
                for n in range(2):
                    w = (a % 2) * HALF_WINDOWS + 2 * p + n
                    made = nc.tensor.matmul(score_bank[64 * n:64 * n + 64, 0:HEADS * TOKENS],
                                            q[:, unit_slot(a), w * TOKENS:(w + 1) * TOKENS],
                                            k_block[:, w, :, :], start=True, stop=True)
                made.then_inc(scores_made, 1)

            def turn_probs(A, a, p):
                pe.wait_ge(probs_ready, PAIRS * A + p + 1)
                wait(pe, probs_t_ready, PAIRS * A + p)
                for m in range(HEAD_PAIRS):
                    made = nc.tensor.transpose(probs_t_bank[:, m * 128:(m + 1) * 128],
                                               probs[:, p, 2 * m:2 * m + 2, :], ident_sb[:, :])
                made.then_inc(probs_turned, 1)

            def times_v(A, a, p):
                if p == 0:
                    pe.wait_ge(v_ready, A + 1)
                    wait(pe, attended_ready, A)
                pe.wait_ge(probs_t_ready, PAIRS * A + p + 1)
                for n in range(2):
                    w = (a % 2) * HALF_WINDOWS + 2 * p + n
                    for m in range(HEAD_PAIRS):
                        first = (2 * p + n) * TOKENS
                        made = nc.tensor.matmul(pv_bank[32 * m:32 * m + 32, first:first + TOKENS],
                                                v_block[:, w, m, :],
                                                probs_t[:, a % 2, m, p, n * TOKENS:(n + 1) * TOKENS],
                                                start=True, stop=True)
                made.then_inc(pv_made, 1)

            def sum_probs(A, a):
                wait(pe, log_sum_made, A)
                for m in range(HEAD_PAIRS):
                    made = nc.tensor.matmul(sum_bank[32 * m:32 * m + 32, :], ones_pair_sb[:, :],
                                            probs_t[:, a % 2, m, :, :], start=True, stop=True)
                made.then_inc(sums_made, 1)

            def project(A, a):
                pe.wait_ge(attended_ready, A + 1)
                mm_wait("proj", A)
                nc.tensor.matmul(mm_bank("proj", a)[0:DIM, :], wproj[:, :], half_of(attended, a),
                                 start=True, stop=True).then_inc(proj_made, 1)

            def mlp_up(A, a, n):
                if n == 0:
                    pe.wait_ge(y_ready[1], A + 1)
                mm_wait(f"mlp1_{n}", A)
                nc.tensor.matmul(mm_bank(f"mlp1_{n}", a)[:, :], w1[:, n * 128:(n + 1) * 128],
                                 half_of(y2, a), start=True, stop=True).then_inc(mlp1_made, 1)

            def mlp_down(A, a, n):
                if n == 0:
                    pe.wait_ge(gelu_ready, HID_CHUNKS * (A + 1))
                    mm_wait("mlp2", A)
                made = nc.tensor.matmul(mm_bank("mlp2", a)[0:DIM, :], w2[:, n, :],
                                        half_of(hidden[:, n, :], a),
                                        start=(n == 0), stop=(n == HID_CHUNKS - 1))
                if n == HID_CHUNKS - 1:
                    made.then_inc(mlp2_made, 1)

            def denominators(A, a):
                pe.wait_ge(sq_ready, A + 1)
                mm_wait("den", A)
                nc.tensor.matmul(mm_bank("den", a)[0:DIM, :], wgdn[:, :], half_of(x3_sq, a),
                                 start=True, stop=True).then_inc(den_made, 1)

            def steps(run):
                run(scores, ATTEND, 0)
                run(turn_probs, ATTEND - 1, 2)
                run(turn_in, MLP, 1)
                run(project_v, ATTEND)
                run(times_v, ATTEND - 1, 2)
                run(project_q, QK)
                run(scores, ATTEND, 1)
                run(turn_probs, ATTEND - 1, 3)
                run(mlp_down, SETTLE, 0)
                run(times_v, ATTEND - 1, 3)
                run(sum_probs, ATTEND - 1)
                for n in range(1, HID_CHUNKS):
                    run(mlp_down, SETTLE, n)
                run(turn_out, TURN_OUT, 0)
                run(scores, ATTEND, 2)
                run(turn_probs, ATTEND, 0)
                run(turn_out, MLP, 1)
                run(project_k, QK)
                run(times_v, ATTEND, 0)
                run(denominators, SETTLE)
                run(project, PROJECT)
                run(scores, ATTEND, 3)
                run(turn_in, TURN_IN, 0)
                run(turn_probs, ATTEND, 1)
                run(mlp_up, MLP, 0)
                run(times_v, ATTEND, 1)
                for n in range(1, HID_CHUNKS):
                    run(mlp_up, MLP, n)

            rounds(pe, steps)


def kernel(x, L0_conv_norm1_w, L0_conv_norm1_b, L0_conv_qkv_w, L0_conv_qkv_b, L0_conv_proj_w,
           L0_conv_proj_b, L0_conv_norm2_w, L0_conv_norm2_b, L0_conv_mlp_w1, L0_conv_mlp_b1,
           L0_conv_mlp_w2, L0_conv_mlp_b2, L1_conv_beta, L1_conv_gamma):
    import numpy as np
    import concourse.bacc as bacc
    from concourse.bass_utils import run_bass_kernel_spmd

    low, right = (np.arange(TOKENS) // WIN >= SHIFT).astype(int), (np.arange(TOKENS) % WIN >= SHIFT).astype(int)
    quadrant = 2 * low + right
    is_in = (quadrant[None, :] == np.arange(4)[:, None]).astype(np.float32)
    qmask = np.zeros((ROWS, MASK_ROWS, WINDOWS, TOKENS), np.float32)
    qmask[:ROWS - 1, 0:4] = is_in[None, :, None, :]
    qmask[ROWS - 1, 4:8] = is_in[:, None, :]
    side_differs = (np.arange(4)[:, None] % 2 != right[None, :])
    height_differs = (np.arange(4)[:, None] // 2 != low[None, :])
    kmask = np.zeros((MASK_ROWS, WINDOWS, HEADS, TOKENS), np.float32)
    kmask[0:4, WINDOWS - 1] = np.where(side_differs, MASKED, 0.0)[:, None, :]
    kmask[4:8, :WINDOWS - 1] = np.where(height_differs, MASKED, 0.0)[:, None, None, :]
    kmask[4:8, WINDOWS - 1] = np.where(side_differs | height_differs, MASKED, 0.0)[:, None, :]
    head_mask = (np.arange(DIM)[:, None] // HEAD_DIM == np.arange(HEADS)[None, :]).astype(np.float32)
    ones_pair = (np.arange(128)[:, None] // 64 == np.arange(32)[None, :] // HEAD_DIM).astype(np.float32)

    col, row = (-1, 1), (1, -1)
    arrays = {
        "x": x, "qmask": qmask.reshape(ROWS, MASK_ROWS, UNIT), "kmask": kmask.reshape(MASK_ROWS, -1),
        "ident": np.eye(128, dtype=np.float32), "head_mask": head_mask, "ones_pair": ones_pair,
        "norm1_w": np.reshape(L0_conv_norm1_w, col), "norm1_b": np.reshape(L0_conv_norm1_b, col),
        "qkv_t": np.transpose(L0_conv_qkv_w), "qkv_b": np.reshape(L0_conv_qkv_b, row),
        "proj_t": np.transpose(L0_conv_proj_w), "proj_b": np.reshape(L0_conv_proj_b, row),
        "norm2_w": np.reshape(L0_conv_norm2_w, col), "norm2_b": np.reshape(L0_conv_norm2_b, col),
        "w1_t": np.transpose(L0_conv_mlp_w1), "b1": np.reshape(L0_conv_mlp_b1, row),
        "w2_t": np.transpose(L0_conv_mlp_w2), "b2": np.reshape(L0_conv_mlp_b2, col),
        "beta": np.reshape(L1_conv_beta, row), "gamma_t": np.transpose(L1_conv_gamma),
    }
    nc = bacc.Bacc("TRN2", target_bir_lowering=False, num_devices=1)
    sent, aps = {}, {}
    for name, a in arrays.items():
        a = np.ascontiguousarray(a)
        sent[f"in_{name}"] = a
        aps[name] = nc.dram_tensor(f"in_{name}", a.shape, mybir.dt.from_np(a.dtype),
                                   kind="ExternalInput").ap()
    out = nc.dram_tensor("out_0", (N_IMAGES, DIM, HEIGHT, WIDTH), mybir.dt.float32,
                         kind="ExternalOutput").ap()
    window_block(nc, out=out, **aps)
    result = run_bass_kernel_spmd(nc, [sent], core_ids=[0])
    return result.results[0]["out_0"]
```

```python
import concourse.bass as bass
from concourse import mybir
from contextlib import ExitStack

N_IMAGES, DIM, HEIGHT, WIDTH = 4, 96, 128, 128
HEADS, WIN, SHIFT = 6, 8, 4
HEAD_DIM = DIM // HEADS
HIDDEN = 4 * DIM
HID_CHUNKS = HIDDEN // 128
ROWS = HEIGHT // WIN
WINDOWS = WIDTH // WIN
TOKENS = WIN * WIN
UNIT = WINDOWS * TOKENS
UNITS = N_IMAGES * ROWS
HALF = UNIT // 2
HALVES = 2 * UNITS
HALF_WINDOWS = WINDOWS // 2
PAIRS = HALF_WINDOWS // 2
HEAD_PAIRS = HEADS // 2
CHUNKS = HALF // 128
MASK_ROWS = 8
LN_EPS = 1e-5
PEDESTAL = 2.0 ** -36
BOUND_BETA = (1e-6 + PEDESTAL) ** 0.5
BOUND_GAMMA = PEDESTAL ** 0.5
MASKED = -100.0
X_SLOTS = 4
TURN_IN, TURN_OUT, QK, ATTEND, PROJECT, MLP, SETTLE, DIVIDE = 4, 3, 1, 0, -1, -2, -3, -4


def window_block(nc, x, qmask, kmask, ident, head_mask, ones_pair, norm1_w, norm1_b, qkv_t, qkv_b,
                 proj_t, proj_b, norm2_w, norm2_b, w1_t, b1, w2_t, b2, beta, gamma_t, out):
    f32 = mybir.dt.float32
    f32r = mybir.dt.float32r
    ALU = mybir.AluOpType
    ACT = mybir.ActivationFunctionType
    AX = mybir.AxisListType

    ctx = ExitStack()
    with ctx:
        def sb(name, shape, dt=f32):
            return ctx.enter_context(nc.sbuf_tensor(name, shape, dt))

        def bank(name):
            return ctx.enter_context(nc.psum_tensor(name, [128, 512], f32))

        def sem(name):
            return ctx.enter_context(nc.semaphore(name))

        ident_sb = sb("ident_sb", [128, 128])
        head_mask_sb = sb("head_mask_sb", [DIM, HEADS])
        ones_pair_sb = sb("ones_pair_sb", [128, 32])
        qkv_raw = sb("qkv_raw", [DIM, 3 * DIM])
        w1_raw = sb("w1_raw", [DIM, HIDDEN])
        norm_cols = sb("norm_cols", [DIM, 4])
        b2_col = sb("b2_col", [DIM, 1])
        wq = sb("wq", [DIM + 1, DIM])
        wk = sb("wk", [DIM + 1, DIM])
        wv = sb("wv", [128, 2, HEAD_PAIRS, HEAD_DIM])
        wproj = sb("wproj", [DIM + 1, DIM])
        w1 = sb("w1", [DIM + 1, HIDDEN])
        w2 = sb("w2", [128, HID_CHUNKS, DIM])
        wq_hi, wq_lo, wk_hi, wk_lo, wproj_hi, wproj_lo, wgdn_hi, wgdn_lo = (
            sb(f"{name}_{part}", [DIM + 1, DIM], f32r)
            for name in ("wq", "wk", "wproj", "wgdn") for part in ("hi", "lo"))
        w1_hi, w1_lo = (sb(f"w1_{part}", [DIM + 1, HIDDEN], f32r) for part in ("hi", "lo"))
        w2_hi, w2_lo = (sb(f"w2_{part}", [128, HID_CHUNKS, DIM], f32r) for part in ("hi", "lo"))
        wgdn = sb("wgdn", [DIM + 1, DIM])
        gdn_raw = sb("gdn_raw", [DIM + 1, DIM])
        qkv_bias = sb("qkv_bias", [DIM + 1, 3 * DIM])
        b1_row = sb("b1_row", [DIM + 1, HIDDEN])
        eps_col = sb("eps_col", [128, 1])

        x_ext = sb("x_ext", [DIM, X_SLOTS, WIN, WIDTH + SHIFT])
        o_ext = sb("o_ext", [DIM, 2, WIN, WIDTH + SHIFT])
        stats = [sb(f"stats{n}", [128, 2 * CHUNKS, 6]) for n in (1, 2)]
        moments = [sb(f"moments{n}", [128, 2 * CHUNKS, 2]) for n in (1, 2)]
        log_var = [sb(f"log_var{n}", [128, 2 * CHUNKS]) for n in (1, 2)]
        rstd = [sb(f"rstd{n}", [128, 2 * CHUNKS]) for n in (1, 2)]
        y_tok = [sb(f"y_tok{n}", [128, 2 * CHUNKS, DIM]) for n in (1, 2)]
        y1 = sb("y1", [128, 2, UNIT])
        y1_hi = sb("y1_hi", [DIM + 1, 2, UNIT], f32r)
        y1_lo = sb("y1_lo", [DIM + 1, 2, UNIT], f32r)
        y2_hi = sb("y2_hi", [DIM + 1, UNIT], f32r)
        y2_lo = sb("y2_lo", [DIM + 1, UNIT], f32r)
        q = sb("q", [128, 2, UNIT])
        k = sb("k", [DIM, UNIT])
        k_block = sb("k_block", [128, WINDOWS, HEADS, TOKENS])
        v_block = sb("v_block", [128, WINDOWS, HEAD_PAIRS, 32])
        row_max = sb("row_max", [128, 2, HEADS])
        shifted = sb("shifted", [128, 2, HEADS, TOKENS])
        probs = sb("probs", [128, 4, HEADS, TOKENS])
        probs_t = sb("probs_t", [128, 2, HEAD_PAIRS, PAIRS, 128])
        log_sum = sb("log_sum", [DIM, HALF])
        inv_sum = sb("inv_sum", [DIM, HALF])
        attended = sb("attended", [DIM, HALF])
        attended_hi = sb("attended_hi", [DIM + 1, HALF], f32r)
        attended_lo = sb("attended_lo", [DIM + 1, HALF], f32r)
        x2 = sb("x2", [DIM, 2, UNIT])
        hidden = sb("hidden", [128, HID_CHUNKS, HALF])
        hidden_hi = sb("hidden_hi", [128, HID_CHUNKS, HALF], f32r)
        hidden_lo = sb("hidden_lo", [128, HID_CHUNKS, HALF], f32r)
        x3 = sb("x3", [DIM, UNIT])
        x3_sq = sb("x3_sq", [DIM, HALF])
        x3_sq_hi = sb("x3_sq_hi", [DIM + 1, HALF], f32r)
        x3_sq_lo = sb("x3_sq_lo", [DIM + 1, HALF], f32r)
        log_den = sb("log_den", [DIM, HALF])
        inv_den = sb("inv_den", [DIM, HALF])

        score_bank = bank("score_bank")
        probs_t_bank = bank("probs_t_bank")
        pv_bank = bank("pv_bank")
        sum_bank = bank("sum_bank")
        turn_banks = [bank("turn_bank1"), bank("turn_bank2")]
        mm_banks = [bank("mm_bank0"), bank("mm_bank1")]

        waits_passed = sem("waits_passed")
        consts_loaded = sem("consts_loaded")
        key_mask_loaded = sem("key_mask_loaded")
        cleared = sem("cleared")
        pads_cleared = sem("pads_cleared")
        weights_folded = sem("weights_folded")
        weights_rounded = sem("weights_rounded")
        bias_products = sem("bias_products")
        x_loaded = [sem(f"x_loaded{n}") for n in range(X_SLOTS)]
        query_mask_loaded = [sem("query_mask_loaded0"), sem("query_mask_loaded1")]
        out_stored = [sem("out_stored0"), sem("out_stored1")]
        x_wrapped = sem("x_wrapped")
        out_wrapped = sem("out_wrapped")
        x_turned = [sem("x_turned1"), sem("x_turned2")]
        stats_made = [sem("stats_made1"), sem("stats_made2")]
        moments_ready = [sem("moments_ready1"), sem("moments_ready2")]
        log_var_made = [sem("log_var_made1"), sem("log_var_made2")]
        rstd_ready = [sem("rstd_ready1"), sem("rstd_ready2")]
        normed = [sem("normed1"), sem("normed2")]
        y_turned = [sem("y_turned1"), sem("y_turned2")]
        y_ready = [sem("y_ready1"), sem("y_ready2")]
        y1_hi_ready = sem("y1_hi_ready")
        y1_split = sem("y1_split")
        y2_split = sem("y2_split")
        q_made = sem("q_made")
        k_made = sem("k_made")
        q_ready = sem("q_ready")
        k_ready = sem("k_ready")
        key_block_v = sem("key_block_v")
        key_block_p = sem("key_block_p")
        v_made = sem("v_made")
        v_ready = sem("v_ready")
        scores_made = sem("scores_made")
        max_ready = sem("max_ready")
        scores_shifted = sem("scores_shifted")
        probs_ready = sem("probs_ready")
        probs_turned = sem("probs_turned")
        probs_t_ready = sem("probs_t_ready")
        pv_made = sem("pv_made")
        sums_made = sem("sums_made")
        log_sum_made = sem("log_sum_made")
        inv_sum_ready = sem("inv_sum_ready")
        attended_ready = sem("attended_ready")
        attended_hi_ready = sem("attended_hi_ready")
        attended_split = sem("attended_split")
        proj_made = sem("proj_made")
        x2_ready = sem("x2_ready")
        mlp1_made = sem("mlp1_made")
        gelu_ready = sem("gelu_ready")
        hidden_hi_ready = sem("hidden_hi_ready")
        hidden_split = sem("hidden_split")
        mlp2_made = sem("mlp2_made")
        x3_ready = sem("x3_ready")
        sq_ready = sem("sq_ready")
        sq_hi_ready = sem("sq_hi_ready")
        sq_split = sem("sq_split")
        den_made = sem("den_made")
        log_den_made = sem("log_den_made")
        inv_den_ready = sem("inv_den_ready")
        out_ready = sem("out_ready")

        def iterations(engine, body):
            first = 4
            trips = (UNITS - 2 - first) // X_SLOTS
            for i in range(-2, first):
                body(i, i % X_SLOTS)
            with engine.Fori(0, trips) as trip:
                for n in range(X_SLOTS):
                    body(X_SLOTS * trip + (first + n), (first + n) % X_SLOTS)
            for i in range(first + X_SLOTS * trips, UNITS + 2):
                body(i, i % X_SLOTS)

        def rounds(engine, steps):
            def body(i, m):
                for n in range(2):
                    H, h = 2 * i + n, 2 * m + n
                    def run(stage, offset, *rest):
                        if has(H + offset):
                            stage(H + offset, (h + offset) % (2 * X_SLOTS), *rest)
                    steps(run)
            iterations(engine, body)

        def has(at, count=HALVES):
            return not isinstance(at, int) or 0 <= at < count

        def wait(engine, semaphore, count):
            if not isinstance(count, int) or count > 0:
                engine.wait_ge(semaphore, count)

        def wait_alone(engine, semaphore, count):
            engine.wait_ge(semaphore, count)
            engine.sem_inc(waits_passed, 1)

        MM_ITEMS = [
            ("v", ATTEND, v_ready, 1, 1), ("den", DIVIDE, log_den_made, 1, 1), ("q", QK, q_ready, 1, 1),
            ("mlp2", SETTLE, x3_ready, 1, 1), ("k", QK, k_ready, 1, 1), ("proj", PROJECT, x2_ready, 1, 1),
            *((f"mlp1_{n}", MLP, gelu_ready, HID_CHUNKS, n + 1) for n in range(HID_CHUNKS)),
        ]
        MM_AT = {item[0]: at for at, item in enumerate(MM_ITEMS)}
        def mm_bank(name, a):
            h = a - MM_ITEMS[MM_AT[name]][1]
            return mm_banks[(MM_AT[name] + len(MM_ITEMS) * h) % 2]

        def mm_bank_emptied(name, A):
            at, H = MM_AT[name], A - MM_ITEMS[MM_AT[name]][1]
            for back in range(1, 2 * len(MM_ITEMS)):
                other = at - 2 * back
                _, offset, semaphore, per_half, own = MM_ITEMS[other % len(MM_ITEMS)]
                B = H + other // len(MM_ITEMS) + offset
                if has(B):
                    return semaphore, per_half * B + own
            return None

        def windows_of(tile, a):
            first = SHIFT + (a % 2) * (WIDTH // 2)
            return tile[:, :, first:first + WIDTH // 2].rearrange("c r (n w) -> c n r w", w=WIN)

        def in_windows(flat):
            return flat.rearrange("c (n r w) -> c n r w", r=WIN, w=WIN)

        def ln_rows(flat, a):
            rows = TOKENS // 2
            return flat.rearrange("c (n t) -> c n t", t=TOKENS)[:, :, (a % 2) * rows:(a % 2 + 1) * rows]

        def half_of(tile, a):
            return tile[:, (a % 2) * HALF:(a % 2 + 1) * HALF]

        def unit_slot(a, slots=2):
            return (a // 2) % slots

        def chunks_of(a):
            return range((a % 2) * CHUNKS, (a % 2 + 1) * CHUNKS)

        def half_windows(a):
            return slice((a % 2) * HALF_WINDOWS, (a % 2 + 1) * HALF_WINDOWS)

        block = ctx.enter_context(nc.Block())

        @block.sync
        def _(sp):
            for dst, src in ((ident_sb[:, :], ident), (head_mask_sb[:, :], head_mask),
                             (ones_pair_sb[:, :], ones_pair), (qkv_raw[:, :], qkv_t),
                             (w1_raw[:, :], w1_t), (norm_cols[:, 0:1], norm1_w),
                             (norm_cols[:, 1:2], norm1_b), (norm_cols[:, 2:3], norm2_w),
                             (norm_cols[:, 3:4], norm2_b), (b2_col[:, :], b2),
                             (wproj[0:DIM, :], proj_t), (wproj[DIM:DIM + 1, :], proj_b),
                             (w2[:, :, :], w2_t.rearrange("(c p) n -> p c n", p=128)),
                             (gdn_raw[0:DIM, :], gamma_t), (gdn_raw[DIM:DIM + 1, :], beta),
                             (qkv_bias[DIM:DIM + 1, :], qkv_b), (b1_row[DIM:DIM + 1, :], b1)):
                sp.dma_start(dst, src).then_inc(consts_loaded, 16)

            def image_rows(unit):
                row = unit % ROWS
                return (0, row * WIN + SHIFT), (SHIFT, ((row + 1) % ROWS) * WIN)

            def load_x(unit, slot):
                for at, first in image_rows(unit):
                    sp.dma_start(x_ext[:, slot, at:at + SHIFT, 0:WIDTH],
                                 x[bass.ds(unit // ROWS, 1), :, bass.ds(first, SHIFT), :]
                                 .rearrange("n c h w -> (n c) h w")).then_inc(x_loaded[slot], 16)

            def load_query_mask(unit, slot):
                sp.dma_start(q[DIM:DIM + MASK_ROWS, slot, :],
                             qmask[bass.ds(unit % ROWS, 1), :, :].rearrange("n m t -> (n m) t"))\
                    .then_inc(query_mask_loaded[slot], 16)

            def store_out(unit, slot):
                for at, first in image_rows(unit):
                    sp.dma_start(out[bass.ds(unit // ROWS, 1), :, bass.ds(first, SHIFT), :]
                                 .rearrange("n c h w -> (n c) h w"),
                                 o_ext[:, slot, at:at + SHIFT, 0:WIDTH])\
                        .then_inc(out_stored[slot], 16)

            def body(i, m):
                if has(i + 2, UNITS):
                    if has(i - 2, UNITS):
                        wait_alone(sp, x2_ready, 2 * (i - 1))
                    load_x(i + 2, (m + 2) % X_SLOTS)
                if has(i + 1, UNITS):
                    if has(i - 1, UNITS):
                        wait_alone(sp, scores_made, 2 * PAIRS * i)
                    elif i == -1:
                        sp.wait_ge(pads_cleared, 1)
                    load_query_mask(i + 1, (m + 1) % 2)
                if has(i - 2, UNITS):
                    wait_alone(sp, out_wrapped, i - 1)
                    store_out(i - 2, m % 2)

            iterations(sp, body)
            for slot in range(2):
                sp.wait_ge(out_stored[slot], 32 * (UNITS // 2))

        @block.gpsimd
        def _(pool):
            nc.gpsimd.memset(q[DIM:128, :, :], 0.0).then_inc(pads_cleared, 1)
            nc.gpsimd.memset(k_block[DIM:128, :, :, :], 0.0).then_inc(pads_cleared, 1)
            pool.wait_ge(pads_cleared, 2)
            pool.dma_start(k_block[DIM:DIM + MASK_ROWS, :, :, :].rearrange("m n h t -> m (n h t)"),
                           kmask).then_inc(key_mask_loaded, 16)
            pool.wait_ge(consts_loaded, 16 * 17)

            def wrap_x(A, a):
                if a % 2 == 0:
                    slot = unit_slot(a, X_SLOTS)
                    wait_alone(pool, x_loaded[slot], 32 * (A // (2 * X_SLOTS) + 1))
                    nc.gpsimd.tensor_copy(x_ext[:, slot, :, WIDTH:WIDTH + SHIFT],
                                          x_ext[:, slot, :, 0:SHIFT]).then_inc(x_wrapped, 2)

            def split(hi, lo, whole, whole_ready, hi_ready, is_split, count):
                wait_alone(pool, whole_ready, count)
                nc.gpsimd.tensor_scalar(hi, whole, 1.0, 1.0, ALU.mult, ALU.mult).then_inc(hi_ready, 1)
                wait_alone(pool, hi_ready, count)
                nc.gpsimd.tensor_tensor(lo, whole, hi, ALU.subtract).then_inc(is_split, 1)

            def split_y1(A, a):
                hi, lo, whole = (ln_rows(tile[0:DIM, unit_slot(a), :], a)
                                 for tile in (y1_hi, y1_lo, y1))
                split(hi, lo, whole, y_ready[0], y1_hi_ready, y1_split, A + 1)

            def split_attended(A, a):
                split(attended_hi[0:DIM, :], attended_lo[0:DIM, :], attended[:, :], attended_ready,
                      attended_hi_ready, attended_split, A + 1)

            def split_squares(A, a):
                split(x3_sq_hi[0:DIM, :], x3_sq_lo[0:DIM, :], x3_sq[:, :], sq_ready,
                      sq_hi_ready, sq_split, A + 1)

            def split_hidden(A, a):
                if has(A - 1):
                    wait_alone(pool, mlp2_made, A)
                for n in range(HID_CHUNKS):
                    split(hidden_hi[:, n, :], hidden_lo[:, n, :], hidden[:, n, :],
                          gelu_ready, hidden_hi_ready, hidden_split, HID_CHUNKS * A + n + 1)

            def key_blocks(A, a):
                wait_alone(pool, k_ready, A + 1)
                for h in range(HEADS // 2):
                    made = nc.gpsimd.tensor_scalar(
                        k_block[0:DIM, half_windows(a), h, :],
                        half_of(k, a).rearrange("c (n t) -> c n t", t=TOKENS),
                        head_mask_sb[:, h:h + 1], 1.0, ALU.mult, ALU.mult)
                made.then_inc(key_block_p, 1)

            def wrap_out(A, a):
                if a % 2 == 1:
                    wait_alone(pool, out_ready, A + 1)
                    slot = unit_slot(a)
                    nc.gpsimd.tensor_copy(o_ext[:, slot, :, 0:SHIFT],
                                          o_ext[:, slot, :, WIDTH:WIDTH + SHIFT]).then_inc(out_wrapped, 1)

            def steps(run):
                run(split_y1, TURN_OUT - 1)
                run(split_hidden, SETTLE)
                run(wrap_x, TURN_IN)
                run(wrap_out, DIVIDE)
                run(split_attended, PROJECT)
                run(split_squares, SETTLE)
                run(key_blocks, QK)

            rounds(pool, steps)

        @block.scalar
        def _(act):
            def rstd_of(A, a, ln):
                act.wait_ge(moments_ready[ln], A + 1)
                cols = slice(chunks_of(a)[0], chunks_of(a)[-1] + 1)
                nc.scalar.activation(log_var[ln][:, cols], moments[ln][:, cols, 1], ACT.Ln,
                                     bias=eps_col[:, :]).then_inc(log_var_made[ln], 1)
                act.wait_ge(log_var_made[ln], A + 1)
                nc.scalar.activation(rstd[ln][:, cols], log_var[ln][:, cols], ACT.Exp, scale=-0.5)\
                    .then_inc(rstd_ready[ln], 1)

            def y_copy(A, a, ln):
                act.wait_ge(y_turned[ln], A + 1)
                if ln == 0:
                    rows = slice(chunks_of(a)[0], chunks_of(a)[-1] + 1)
                    dst = in_windows(y1[0:DIM, unit_slot(a), :])[:, :, rows, :]
                    src = turn_banks[ln][0:DIM, :].rearrange("c (r n w) -> c n r w", r=CHUNKS, w=WIN)
                else:
                    dst, src = half_of(y2_hi[0:DIM, :], a), turn_banks[ln][0:DIM, :]
                nc.scalar.activation(dst, src, ACT.Copy).then_inc(y_ready[ln], 1)

            def q_copy(A, a):
                act.wait_ge(q_made, A + 1)
                nc.scalar.activation(half_of(q[0:DIM, unit_slot(a), :], a), mm_bank("q", a)[0:DIM, :],
                                     ACT.Copy).then_inc(q_ready, 1)

            def k_copy(A, a):
                act.wait_ge(k_made, A + 1)
                wait(act, key_block_v, A - 1)
                wait(act, key_block_p, A - 1)
                nc.scalar.activation(half_of(k, a), mm_bank("k", a)[0:DIM, :], ACT.Copy)\
                    .then_inc(k_ready, 1)

            def softmax_exp(A, a, p):
                pair = PAIRS * A + p
                act.wait_ge(scores_shifted, pair + 1)
                wait(act, probs_turned, pair - 3)
                nc.scalar.activation(probs[:, p, :, :], shifted[:, p % 2, :, :], ACT.Exp)\
                    .then_inc(probs_ready, 1)

            def probs_t_copy(A, a, p):
                act.wait_ge(probs_turned, PAIRS * A + p + 1)
                nc.scalar.activation(probs_t[:, a % 2, :, p, :],
                                     probs_t_bank[:, 0:HEAD_PAIRS * 128]
                                     .rearrange("k (p t) -> k p t", p=HEAD_PAIRS), ACT.Copy)\
                    .then_inc(probs_t_ready, 1)

            def inverse_sums(A, a):
                act.wait_ge(sums_made, A + 1)
                nc.scalar.activation(log_sum[:, :], sum_bank[0:DIM, :], ACT.Ln).then_inc(log_sum_made, 1)
                act.wait_ge(log_sum_made, A + 1)
                wait(act, attended_ready, A)
                nc.scalar.activation(inv_sum[:, :], log_sum[:, :], ACT.Exp, scale=-1.0)\
                    .then_inc(inv_sum_ready, 1)

            def gelus(A, a):
                wait(act, hidden_split, HID_CHUNKS * A)
                for n in range(HID_CHUNKS):
                    act.wait_ge(mlp1_made, HID_CHUNKS * A + n + 1)
                    nc.scalar.activation(hidden[:, n, :], mm_bank(f"mlp1_{n}", a)[:, :],
                                         ACT.Gelu).then_inc(gelu_ready, 1)

            def squares(A, a):
                act.wait_ge(x3_ready, A + 1)
                nc.scalar.activation(x3_sq[:, :], half_of(x3, a), ACT.Square)\
                    .then_inc(sq_ready, 1)

            def log_denominators(A, a):
                act.wait_ge(den_made, A + 1)
                nc.scalar.activation(log_den[:, :], mm_bank("den", a)[0:DIM, :], ACT.Ln)\
                    .then_inc(log_den_made, 1)

            def inverse_denominators(A, a):
                act.wait_ge(log_den_made, A + 1)
                nc.scalar.activation(inv_den[:, :], log_den[:, :], ACT.Exp, scale=-0.5)\
                    .then_inc(inv_den_ready, 1)

            def steps(run):
                run(probs_t_copy, ATTEND - 1, 2)
                nc.scalar.preload_act_table_set("natural_log_exp_and_others")
                run(softmax_exp, ATTEND - 1, 3)
                run(softmax_exp, ATTEND, 0)
                run(rstd_of, TURN_OUT, 0)
                run(log_denominators, DIVIDE)
                run(probs_t_copy, ATTEND - 1, 3)
                run(inverse_denominators, DIVIDE)
                run(rstd_of, MLP, 1)
                run(q_copy, QK)
                run(softmax_exp, ATTEND, 1)
                run(inverse_sums, PROJECT)
                run(y_copy, TURN_OUT, 0)
                run(probs_t_copy, ATTEND, 0)
                run(squares, SETTLE)
                run(y_copy, MLP, 1)
                run(k_copy, QK)
                run(probs_t_copy, ATTEND, 1)
                run(softmax_exp, ATTEND, 2)
                nc.scalar.preload_act_table_set("gelu_and_others")
                run(gelus, MLP)

            rounds(act, steps)

        @block.vector
        def _(dve):
            nc.vector.memset(y1[DIM:128, :, :], 0.0).then_inc(cleared, 1)
            nc.vector.memset(wv[DIM:128, :, :, :], 0.0).then_inc(cleared, 1)
            nc.vector.memset(v_block[:, :, :, :], 0.0).then_inc(cleared, 1)
            nc.vector.memset(eps_col[:, :], LN_EPS).then_inc(cleared, 1)
            dve.wait_ge(cleared, 4)
            nc.vector.memset(y1[DIM:DIM + 1, :, :], 1.0).then_inc(cleared, 1)
            dve.wait_ge(cleared, 5)
            for hi, lo in ((y1_hi[:, 0, :], y1_lo[:, 0, :]), (y1_hi[:, 1, :], y1_lo[:, 1, :]),
                           (y2_hi, y2_lo), (attended_hi, attended_lo), (x3_sq_hi, x3_sq_lo)):
                ones = y1[DIM:DIM + 1, 0, 0:hi.shape[-1]]
                nc.vector.tensor_copy(hi[DIM:DIM + 1, :], ones)
                made = nc.vector.tensor_scalar(lo[DIM:DIM + 1, :], ones, 0.0, None, ALU.mult)
            made.then_inc(cleared, 1)
            dve.wait_ge(consts_loaded, 16 * 17)
            head_scale = HEAD_DIM ** -0.5
            nc.vector.tensor_scalar(wq[0:DIM, :], qkv_raw[:, 0:DIM], norm_cols[:, 0:1], head_scale,
                                    ALU.mult, ALU.mult)
            nc.vector.tensor_scalar(wk[0:DIM, :], qkv_raw[:, DIM:2 * DIM], norm_cols[:, 0:1], None,
                                    ALU.mult)
            def even_odd(row):
                return row.rearrange("c (p e d) -> c e p d", e=2, d=HEAD_DIM)
            nc.vector.tensor_scalar(wv[0:DIM, :, :, :], even_odd(qkv_raw[:, 2 * DIM:3 * DIM]),
                                    norm_cols[:, 0:1], None, ALU.mult)
            nc.vector.tensor_scalar(w1[0:DIM, :], w1_raw[:, :], norm_cols[:, 2:3], None, ALU.mult)
            nc.vector.tensor_scalar(gdn_raw[0:DIM, :], gdn_raw[0:DIM, :], BOUND_GAMMA, None, ALU.max)\
                .then_inc(weights_folded, 1)
            nc.vector.tensor_scalar(gdn_raw[DIM:DIM + 1, :], gdn_raw[DIM:DIM + 1, :], BOUND_BETA, None,
                                    ALU.max).then_inc(weights_folded, 1)
            dve.wait_ge(weights_folded, 2)
            nc.vector.tensor_tensor(wgdn[:, :], gdn_raw[:, :], gdn_raw[:, :], ALU.mult)\
                .then_inc(weights_folded, 1)
            dve.wait_ge(weights_folded, 3)
            nc.vector.tensor_scalar(wgdn[:, :], wgdn[:, :], -PEDESTAL, None, ALU.add)
            dve.wait_ge(bias_products, 1)
            row = slice(DIM, DIM + 1)
            qkv_shift = score_bank[row, 0:3 * DIM]
            nc.vector.tensor_tensor(qkv_bias[row, :], qkv_shift, qkv_bias[row, :], ALU.add)\
                .then_inc(weights_folded, 1)
            nc.vector.tensor_tensor(w1[row, :], pv_bank[row, 0:HIDDEN], b1_row[row, :], ALU.add)\
                .then_inc(weights_folded, 1)
            dve.wait_ge(weights_folded, 5)
            nc.vector.tensor_scalar(wq[row, :], qkv_bias[row, 0:DIM], head_scale, None, ALU.mult)
            nc.vector.tensor_copy(wk[row, :], qkv_bias[row, DIM:2 * DIM]).then_inc(weights_folded, 1)
            nc.vector.tensor_copy(wv[row, :, :, :], even_odd(qkv_bias[row, 2 * DIM:3 * DIM]))
            dve.wait_ge(weights_folded, 6)
            weights_in_parts = ((wq_hi[:, :], wq_lo[:, :], wq[:, :]), (wk_hi[:, :], wk_lo[:, :], wk[:, :]),
                                (wproj_hi[:, :], wproj_lo[:, :], wproj[:, :]),
                                (wgdn_hi[:, :], wgdn_lo[:, :], wgdn[:, :]),
                                (w1_hi[:, :], w1_lo[:, :], w1[:, :]),
                                (w2_hi[:, :, :], w2_lo[:, :, :], w2[:, :, :]))
            for hi, _, whole in weights_in_parts:
                nc.vector.tensor_copy(hi, whole).then_inc(weights_rounded, 1)
            dve.wait_ge(weights_rounded, len(weights_in_parts))
            for hi, lo, whole in weights_in_parts:
                made = nc.vector.tensor_tensor(lo, whole, hi, ALU.subtract)
            made.then_inc(weights_folded, 1)

            def statistics(A, a, ln):
                dve.wait_ge(x_turned[ln], A + 1)
                for n, c in enumerate(chunks_of(a)):
                    made = nc.vector.bn_stats(stats[ln][:, c, :],
                                              turn_banks[ln][:, n * DIM:(n + 1) * DIM])
                made.then_inc(stats_made[ln], 1)
                wait_alone(dve, stats_made[ln], A + 1)
                for c in chunks_of(a):
                    made = nc.vector.bn_aggr(moments[ln][:, c, :], stats[ln][:, c, :])
                made.then_inc(moments_ready[ln], 1)

            def normalise(A, a, ln):
                dve.wait_ge(rstd_ready[ln], A + 1)
                for n, c in enumerate(chunks_of(a)):
                    made = nc.vector.tensor_scalar(y_tok[ln][:, c, :],
                                                   turn_banks[ln][:, n * DIM:(n + 1) * DIM],
                                                   moments[ln][:, c, 0:1], rstd[ln][:, c:c + 1],
                                                   ALU.subtract, ALU.mult)
                made.then_inc(normed[ln], 1)

            def split_y2(A, a):
                dve.wait_ge(y_ready[1], A + 1)
                nc.vector.tensor_tensor(half_of(y2_lo[0:DIM, :], a), turn_banks[1][0:DIM, :],
                                        half_of(y2_hi[0:DIM, :], a), ALU.subtract).then_inc(y2_split, 1)

            def key_blocks(A, a):
                dve.wait_ge(k_ready, A + 1)
                for h in range(HEADS // 2, HEADS):
                    made = nc.vector.tensor_scalar(
                        k_block[0:DIM, half_windows(a), h, :],
                        half_of(k, a).rearrange("c (n t) -> c n t", t=TOKENS),
                        head_mask_sb[:, h:h + 1], None, ALU.mult)
                made.then_inc(key_block_v, 1)

            def v_blocks(A, a):
                dve.wait_ge(v_made, A + 1)
                for e in range(2):
                    rows = slice(64 * e, 64 * e + 64)
                    made = nc.vector.tensor_copy(
                        v_block[rows, half_windows(a), :, HEAD_DIM * e:HEAD_DIM * (e + 1)],
                        mm_bank("v", a)[rows, 0:HALF_WINDOWS * HEAD_PAIRS * HEAD_DIM]
                        .rearrange("k (n p d) -> k n p d", n=HALF_WINDOWS, p=HEAD_PAIRS))
                made.then_inc(v_ready, 1)

            def shift_scores(A, a, p):
                pair = PAIRS * A + p
                dve.wait_ge(scores_made, pair + 1)
                scores = score_bank[:, 0:HEADS * TOKENS].rearrange("t (h k) -> t h k", h=HEADS)
                nc.vector.tensor_reduce(row_max[:, p % 2, :], scores, op=ALU.max, axis=AX.X)\
                    .then_inc(max_ready, 1)
                dve.wait_ge(max_ready, pair + 1)
                wait(dve, probs_ready, pair - 1)
                nc.vector.tensor_tensor(shifted[:, p % 2, :, :], scores,
                                        row_max[:, p % 2, :].unsqueeze(2)
                                        .broadcast_to([128, HEADS, TOKENS]), ALU.subtract)\
                    .then_inc(scores_shifted, 1)

            def divide(A, a):
                dve.wait_ge(inv_sum_ready, A + 1)
                dve.wait_ge(pv_made, PAIRS * (A + 1))
                nc.vector.tensor_tensor(attended[:, :], pv_bank[0:DIM, :],
                                        inv_sum[:, :], ALU.mult).then_inc(attended_ready, 1)

            def first_residual(A, a):
                dve.wait_ge(proj_made, A + 1)
                nc.vector.tensor_tensor(in_windows(half_of(x2[:, unit_slot(a), :], a)),
                                        in_windows(mm_bank("proj", a)[0:DIM, :]),
                                        windows_of(x_ext[:, unit_slot(a, X_SLOTS), :, :], a), ALU.add)\
                    .then_inc(x2_ready, 1)

            def second_residual(A, a):
                dve.wait_ge(mlp2_made, A + 1)
                nc.vector.scalar_tensor_tensor(half_of(x3, a), mm_bank("mlp2", a)[0:DIM, :],
                                               b2_col[:, :], half_of(x2[:, unit_slot(a), :], a),
                                               ALU.add, ALU.add).then_inc(x3_ready, 1)

            def outputs(A, a):
                dve.wait_ge(inv_den_ready, A + 1)
                wait(dve, out_stored[unit_slot(a)], 32 * (A // 4))
                nc.vector.tensor_tensor(windows_of(o_ext[:, unit_slot(a), :, :], a),
                                        in_windows(half_of(x3, a)), in_windows(inv_den[:, :]),
                                        ALU.mult).then_inc(out_ready, 1)

            def steps(run):
                run(shift_scores, ATTEND, 0)
                run(v_blocks, ATTEND)
                run(statistics, MLP, 1)
                run(normalise, TURN_OUT, 0)
                run(shift_scores, ATTEND, 1)
                run(normalise, MLP, 1)
                run(outputs, DIVIDE)
                run(divide, PROJECT)
                run(second_residual, SETTLE)
                run(shift_scores, ATTEND, 2)
                run(split_y2, MLP)
                run(shift_scores, ATTEND, 3)
                run(first_residual, PROJECT)
                run(key_blocks, QK)
                run(statistics, TURN_IN, 0)

            rounds(dve, steps)

        @block.tensor
        def _(pe):
            pe.wait_ge(consts_loaded, 16 * 17)
            row = slice(DIM, DIM + 1)
            nc.tensor.matmul(score_bank[row, 0:3 * DIM], norm_cols[:, 1:2], qkv_raw[:, :],
                             start=True, stop=True)
            nc.tensor.matmul(pv_bank[row, 0:HIDDEN], norm_cols[:, 3:4], w1_raw[:, :],
                             start=True, stop=True).then_inc(bias_products, 1)
            pe.wait_ge(weights_folded, 7)
            pe.wait_ge(cleared, 6)
            pe.wait_ge(pads_cleared, 2)
            pe.wait_ge(key_mask_loaded, 16)

            def mm_wait(name, A):
                found = mm_bank_emptied(name, A)
                if found is not None:
                    wait(pe, *found)

            def turn_in(A, a, ln):
                if ln == 0:
                    pe.wait_ge(x_wrapped, A + 1)
                else:
                    pe.wait_ge(x2_ready, A + 1)
                wait(pe, (y_ready[0], y2_split)[ln], A)
                for n, c in enumerate(chunks_of(a)):
                    if ln == 0:
                        chunk = x_ext[:, unit_slot(a, X_SLOTS), c, SHIFT:SHIFT + WIDTH]
                    else:
                        chunk = x2[:, unit_slot(a), c * 128:(c + 1) * 128]
                    made = nc.tensor.transpose(turn_banks[ln][:, n * DIM:(n + 1) * DIM], chunk,
                                               ident_sb[0:DIM, 0:DIM])
                made.then_inc(x_turned[ln], 1)

            def turn_out(A, a, ln):
                pe.wait_ge(normed[ln], A + 1)
                for n, c in enumerate(chunks_of(a)):
                    made = nc.tensor.transpose(turn_banks[ln][0:DIM, n * 128:(n + 1) * 128],
                                               y_tok[ln][:, c, :], ident_sb[:, :])
                made.then_inc(y_turned[ln], 1)

            def in_parts(out, w_hi, w_lo, hi, lo, first=True, last=True):
                for part, (w, x_part) in enumerate(((w_hi, hi), (w_lo, hi), (w_hi, lo))):
                    made = nc.tensor.matmul(out, w, x_part, start=first and part == 0,
                                            stop=last and part == 2)
                return made

            def project_q(A, a):
                pe.wait_ge(y1_split, A + 2 - a % 2)
                mm_wait("q", A)
                in_parts(mm_bank("q", a)[0:DIM, :], wq_hi[:, :], wq_lo[:, :],
                         half_of(y1_hi[:, unit_slot(a), :], a), half_of(y1_lo[:, unit_slot(a), :], a))\
                    .then_inc(q_made, 1)

            def project_k(A, a):
                mm_wait("k", A)
                in_parts(mm_bank("k", a)[0:DIM, :], wk_hi[:, :], wk_lo[:, :],
                         half_of(y1_hi[:, unit_slot(a), :], a), half_of(y1_lo[:, unit_slot(a), :], a))\
                    .then_inc(k_made, 1)

            def project_v(A, a):
                mm_wait("v", A)
                width = HEAD_PAIRS * HEAD_DIM
                for n in range(HALF_WINDOWS):
                    tokens = half_of(y1[:, unit_slot(a), :], a)[:, n * TOKENS:(n + 1) * TOKENS]
                    for e in range(2):
                        made = nc.tensor.matmul(mm_bank("v", a)[64 * e:64 * e + 64,
                                                             n * width:(n + 1) * width],
                                                tokens, wv[:, e, :, :], start=True, stop=True)
                made.then_inc(v_made, 1)

            def scores(A, a, p):
                if p == 0:
                    pe.wait_ge(q_ready, A + 1)
                    pe.wait_ge(query_mask_loaded[unit_slot(a)], 16 * (A // 4 + 1))
                    pe.wait_ge(key_block_v, A + 1)
                    pe.wait_ge(key_block_p, A + 1)
                wait(pe, scores_shifted, PAIRS * A + p)
                for n in range(2):
                    w = (a % 2) * HALF_WINDOWS + 2 * p + n
                    made = nc.tensor.matmul(score_bank[64 * n:64 * n + 64, 0:HEADS * TOKENS],
                                            q[:, unit_slot(a), w * TOKENS:(w + 1) * TOKENS],
                                            k_block[:, w, :, :], start=True, stop=True)
                made.then_inc(scores_made, 1)

            def turn_probs(A, a, p):
                pe.wait_ge(probs_ready, PAIRS * A + p + 1)
                wait(pe, probs_t_ready, PAIRS * A + p)
                for m in range(HEAD_PAIRS):
                    made = nc.tensor.transpose(probs_t_bank[:, m * 128:(m + 1) * 128],
                                               probs[:, p, 2 * m:2 * m + 2, :], ident_sb[:, :])
                made.then_inc(probs_turned, 1)

            def times_v(A, a, p):
                if p == 0:
                    pe.wait_ge(v_ready, A + 1)
                    wait(pe, attended_ready, A)
                pe.wait_ge(probs_t_ready, PAIRS * A + p + 1)
                for n in range(2):
                    w = (a % 2) * HALF_WINDOWS + 2 * p + n
                    for m in range(HEAD_PAIRS):
                        first = (2 * p + n) * TOKENS
                        made = nc.tensor.matmul(pv_bank[32 * m:32 * m + 32, first:first + TOKENS],
                                                v_block[:, w, m, :],
                                                probs_t[:, a % 2, m, p, n * TOKENS:(n + 1) * TOKENS],
                                                start=True, stop=True)
                made.then_inc(pv_made, 1)

            def sum_probs(A, a):
                wait(pe, log_sum_made, A)
                for m in range(HEAD_PAIRS):
                    made = nc.tensor.matmul(sum_bank[32 * m:32 * m + 32, :], ones_pair_sb[:, :],
                                            probs_t[:, a % 2, m, :, :], start=True, stop=True)
                made.then_inc(sums_made, 1)

            def project(A, a):
                pe.wait_ge(attended_split, A + 1)
                mm_wait("proj", A)
                in_parts(mm_bank("proj", a)[0:DIM, :], wproj_hi[:, :], wproj_lo[:, :],
                         attended_hi[:, :], attended_lo[:, :]).then_inc(proj_made, 1)

            def mlp_up(A, a, n):
                if n == 0:
                    pe.wait_ge(y2_split, A + 1)
                mm_wait(f"mlp1_{n}", A)
                cols = slice(n * 128, (n + 1) * 128)
                in_parts(mm_bank(f"mlp1_{n}", a)[:, :], w1_hi[:, cols], w1_lo[:, cols],
                         half_of(y2_hi, a), half_of(y2_lo, a)).then_inc(mlp1_made, 1)

            def mlp_down(A, a, n):
                if n == 0:
                    mm_wait("mlp2", A)
                pe.wait_ge(hidden_split, HID_CHUNKS * A + n + 1)
                made = in_parts(mm_bank("mlp2", a)[0:DIM, :], w2_hi[:, n, :], w2_lo[:, n, :],
                                hidden_hi[:, n, :], hidden_lo[:, n, :],
                                first=(n == 0), last=(n == HID_CHUNKS - 1))
                if n == HID_CHUNKS - 1:
                    made.then_inc(mlp2_made, 1)

            def denominators(A, a):
                pe.wait_ge(sq_split, A + 1)
                mm_wait("den", A)
                in_parts(mm_bank("den", a)[0:DIM, :], wgdn_hi[:, :], wgdn_lo[:, :],
                         x3_sq_hi[:, :], x3_sq_lo[:, :]).then_inc(den_made, 1)

            def steps(run):
                run(turn_probs, ATTEND - 1, 2)
                run(turn_in, MLP, 1)
                run(scores, ATTEND, 0)
                run(project_v, ATTEND)
                run(times_v, ATTEND - 1, 2)
                run(denominators, DIVIDE)
                run(turn_probs, ATTEND - 1, 3)
                run(scores, ATTEND, 1)
                run(project_q, QK)
                run(times_v, ATTEND - 1, 3)
                run(sum_probs, ATTEND - 1)
                for n in range(HID_CHUNKS):
                    run(mlp_down, SETTLE, n)
                run(turn_out, TURN_OUT, 0)
                run(scores, ATTEND, 2)
                run(turn_probs, ATTEND, 0)
                run(turn_out, MLP, 1)
                run(project_k, QK)
                run(times_v, ATTEND, 0)
                run(turn_probs, ATTEND, 1)
                run(scores, ATTEND, 3)
                run(turn_in, TURN_IN, 0)
                run(project, PROJECT)
                run(mlp_up, MLP, 0)
                run(times_v, ATTEND, 1)
                run(mlp_up, MLP, 1)
                run(mlp_up, MLP, 2)

            rounds(pe, steps)


def kernel(x, L0_conv_norm1_w, L0_conv_norm1_b, L0_conv_qkv_w, L0_conv_qkv_b, L0_conv_proj_w,
           L0_conv_proj_b, L0_conv_norm2_w, L0_conv_norm2_b, L0_conv_mlp_w1, L0_conv_mlp_b1,
           L0_conv_mlp_w2, L0_conv_mlp_b2, L1_conv_beta, L1_conv_gamma):
    import numpy as np
    import concourse.bacc as bacc
    from concourse.bass_utils import run_bass_kernel_spmd

    low, right = (np.arange(TOKENS) // WIN >= SHIFT).astype(int), (np.arange(TOKENS) % WIN >= SHIFT).astype(int)
    quadrant = 2 * low + right
    is_in = (quadrant[None, :] == np.arange(4)[:, None]).astype(np.float32)
    qmask = np.zeros((ROWS, MASK_ROWS, WINDOWS, TOKENS), np.float32)
    qmask[:ROWS - 1, 0:4] = is_in[None, :, None, :]
    qmask[ROWS - 1, 4:8] = is_in[:, None, :]
    side_differs = (np.arange(4)[:, None] % 2 != right[None, :])
    height_differs = (np.arange(4)[:, None] // 2 != low[None, :])
    kmask = np.zeros((MASK_ROWS, WINDOWS, HEADS, TOKENS), np.float32)
    kmask[0:4, WINDOWS - 1] = np.where(side_differs, MASKED, 0.0)[:, None, :]
    kmask[4:8, :WINDOWS - 1] = np.where(height_differs, MASKED, 0.0)[:, None, None, :]
    kmask[4:8, WINDOWS - 1] = np.where(side_differs | height_differs, MASKED, 0.0)[:, None, :]
    head_mask = (np.arange(DIM)[:, None] // HEAD_DIM == np.arange(HEADS)[None, :]).astype(np.float32)
    ones_pair = (np.arange(128)[:, None] // 64 == np.arange(32)[None, :] // HEAD_DIM).astype(np.float32)

    col, row = (-1, 1), (1, -1)
    arrays = {
        "x": x, "qmask": qmask.reshape(ROWS, MASK_ROWS, UNIT), "kmask": kmask.reshape(MASK_ROWS, -1),
        "ident": np.eye(128, dtype=np.float32), "head_mask": head_mask, "ones_pair": ones_pair,
        "norm1_w": np.reshape(L0_conv_norm1_w, col), "norm1_b": np.reshape(L0_conv_norm1_b, col),
        "qkv_t": np.transpose(L0_conv_qkv_w), "qkv_b": np.reshape(L0_conv_qkv_b, row),
        "proj_t": np.transpose(L0_conv_proj_w), "proj_b": np.reshape(L0_conv_proj_b, row),
        "norm2_w": np.reshape(L0_conv_norm2_w, col), "norm2_b": np.reshape(L0_conv_norm2_b, col),
        "w1_t": np.transpose(L0_conv_mlp_w1), "b1": np.reshape(L0_conv_mlp_b1, row),
        "w2_t": np.transpose(L0_conv_mlp_w2), "b2": np.reshape(L0_conv_mlp_b2, col),
        "beta": np.reshape(L1_conv_beta, row), "gamma_t": np.transpose(L1_conv_gamma),
    }
    nc = bacc.Bacc("TRN2", target_bir_lowering=False, num_devices=1)
    sent, aps = {}, {}
    for name, a in arrays.items():
        a = np.ascontiguousarray(a)
        sent[f"in_{name}"] = a
        aps[name] = nc.dram_tensor(f"in_{name}", a.shape, mybir.dt.from_np(a.dtype),
                                   kind="ExternalInput").ap()
    out = nc.dram_tensor("out_0", (N_IMAGES, DIM, HEIGHT, WIDTH), mybir.dt.float32,
                         kind="ExternalOutput").ap()
    window_block(nc, out=out, **aps)
    result = run_bass_kernel_spmd(nc, [sent], core_ids=[0])
    return result.results[0]["out_0"]
```
